# Optimizing a Trainium2 kernel written in Bass

```python
import numpy as np
import jax
import jax.numpy as jnp

def _softmax(x, axis=-1):
    return jax.nn.softmax(x, axis=axis)

def _gelu(x):
    return jax.nn.gelu(x, approximate=True)

def _silu(x):
    return jax.nn.silu(x)

def _sigmoid(x):
    return jax.nn.sigmoid(x)

def _layernorm(x, axis=-1, eps=1e-05):
    m = jnp.mean(x, axis=axis, keepdims=True)
    v = jnp.var(x, axis=axis, keepdims=True)
    return (x - m) / jnp.sqrt(v + eps)

def _scatter_add(tgt, idx, src, axis=0):
    return tgt.at[idx].add(src)

def _segment_sum(src, seg, n):
    return jax.ops.segment_sum(src, seg, n)
kernel_name = 'mk_seq_preln_d4_jaxref_r8_244b53'

def setup_inputs(seed: int=0):
    np.random.seed(seed)
    _w = jnp.asarray

    def _L0_attn_setup():
        import jax, jax.numpy as jnp
        import numpy as np
        B, T, D = (4, 256, 128)
        H, Dh = (16, 64)
        key = jax.random.key(seed)
        ks = jax.random.split(key, 5)
        std_qkv = float(np.sqrt(2.0 / (Dh * D)))
        std_o = float(np.sqrt(2.0 / (D * Dh)))
        return {'x': jax.random.normal(ks[0], (B, T, D), dtype=jnp.float32), 'W_Q': jax.random.normal(ks[1], (H, Dh, D), dtype=jnp.float32) * std_qkv, 'b_Q': jnp.zeros((H, Dh), dtype=jnp.float32), 'W_K': jax.random.normal(ks[2], (H, Dh, D), dtype=jnp.float32) * std_qkv, 'b_K': jnp.zeros((H, Dh), dtype=jnp.float32), 'W_V': jax.random.normal(ks[3], (H, Dh, D), dtype=jnp.float32) * std_qkv, 'b_V': jnp.zeros((H, Dh), dtype=jnp.float32), 'W_O': jax.random.normal(ks[4], (H, D, Dh), dtype=jnp.float32) * std_o, 'b_O': jnp.zeros((D,), dtype=jnp.float32)}
    _L0_attn_in = _L0_attn_setup()

    def _L0_ffn_setup():
        import jax, jax.numpy as jnp
        import numpy as np
        H = 128
        E = 8
        B, S = (4, 256)
        key = jax.random.key(seed)
        k1, k2, k3, k4 = jax.random.split(key, 4)
        x = jax.random.normal(k1, (B, S, H), dtype=jnp.float32)
        wg = jax.random.normal(k2, (H, E), dtype=jnp.float32) * 0.02
        W = jax.random.normal(k3, (E, H, H), dtype=jnp.float32) * 0.02
        b = jax.random.normal(k4, (E, H), dtype=jnp.float32) * 0.02
        return {'x': x, 'wg': wg, 'W': W, 'b': b}
    _L0_ffn_in = _L0_ffn_setup()

    def _L1_attn_setup():
        import jax, jax.numpy as jnp
        import numpy as np
        EMB, HEADS, HIDDEN = (128, 16, 64)
        BS, N = (2, 256)
        key = jax.random.key(seed)
        ks = jax.random.split(key, 7)
        s_in = 1.0 / np.sqrt(EMB)
        s_u = 1.0 / np.sqrt(HEADS * HIDDEN)
        return {'x': jax.random.normal(ks[0], (BS, N, EMB), dtype=jnp.float32), 'w_q': jax.random.uniform(ks[1], (EMB, HEADS * HIDDEN), jnp.float32, -s_in, s_in), 'w_k': jax.random.uniform(ks[2], (EMB, HEADS * HIDDEN), jnp.float32, -s_in, s_in), 'w_v': jax.random.uniform(ks[3], (EMB, HEADS * HIDDEN), jnp.float32, -s_in, s_in), 'w_u': jax.random.uniform(ks[4], (HEADS * HIDDEN, EMB), jnp.float32, -s_u, s_u), 'b_u': jax.random.uniform(ks[5], (EMB,), jnp.float32, -s_u, s_u)}
    _L1_attn_in = _L1_attn_setup()

    def _L1_ffn_setup():
        import jax, jax.numpy as jnp
        import numpy as np
        DIM = 128

        def _reference_tuple_inner(x, W_r, W_k, W_v, mu_r, mu_k):
            B, T, C = x.shape
            x_prev = jnp.concatenate([jnp.zeros((B, 1, C), x.dtype), x[:, :-1, :]], axis=1)
            xr = mu_r * x + (1.0 - mu_r) * x_prev
            xk = mu_k * x + (1.0 - mu_k) * x_prev
            r = jax.nn.sigmoid(jnp.einsum('btc,dc->btd', xr, W_r))
            k = jnp.einsum('btc,dc->btd', xk, W_k)
            k_act = jnp.square(jax.nn.relu(k))
            out = r * jnp.einsum('btc,dc->btd', k_act, W_v)
            new_state = x[:, -1, :]
            return (out, new_state)
        key = jax.random.key(seed)
        ks = jax.random.split(key, 6)
        B, T, C = (8, 256, DIM)
        x = jax.random.normal(ks[0], (B, T, C), dtype=jnp.float32)
        s = 1.0 / np.sqrt(C)
        W_r = jax.random.uniform(ks[1], (C, C), jnp.float32, -s, s)
        W_k = jax.random.uniform(ks[2], (C, C), jnp.float32, -s, s)
        W_v = jax.random.uniform(ks[3], (C, C), jnp.float32, -s, s)
        mu_r = jax.random.uniform(ks[4], (C,), jnp.float32)
        mu_k = jax.random.uniform(ks[5], (C,), jnp.float32)
        return {'x': x, 'W_r': W_r, 'W_k': W_k, 'W_v': W_v, 'mu_r': mu_r, 'mu_k': mu_k}
    _L1_ffn_in = _L1_ffn_setup()

    def _L2_attn_setup():
        import jax, jax.numpy as jnp
        import numpy as np
        import math
        T, N, D, H = (256, 2, 128, 16)
        HD = D // H
        key = jax.random.key(seed)
        k1, k2, k3, k4, k5 = jax.random.split(key, 5)
        scale = 0.02
        return {'x': jax.random.normal(k1, (T, N, D), dtype=jnp.float32), 'q_weight': jax.random.normal(k2, (D, H, HD), dtype=jnp.float32) * scale, 'v_weight': jax.random.normal(k3, (D, H, HD), dtype=jnp.float32) * scale, 'out_w': jax.random.normal(k4, (D, D), dtype=jnp.float32) * scale, 'out_b': jax.random.normal(k5, (D,), dtype=jnp.float32) * scale}
    _L2_attn_in = _L2_attn_setup()

    def _L2_ffn_setup():
        import jax, jax.numpy as jnp
        import numpy as np
        EPS = 1e-05

        def _quantize(W):
            gamma = jnp.mean(jnp.abs(W))
            return jnp.clip(jnp.round(W / (gamma + EPS)), -1.0, 1.0)
        key = jax.random.key(seed)
        k_x, k_w1, k_b1, k_w2, k_b2 = jax.random.split(key, 5)
        n_embd = 128
        d_ff = 4 * n_embd
        B, S = (4, 512)
        bound1 = 1.0 / np.sqrt(n_embd)
        bound2 = 1.0 / np.sqrt(d_ff)
        x = jax.random.normal(k_x, (B, S, n_embd), dtype=jnp.float32)
        W1 = jax.random.uniform(k_w1, (d_ff, n_embd), jnp.float32, -bound1, bound1)
        b1 = jax.random.uniform(k_b1, (d_ff,), jnp.float32, -bound1, bound1)
        W2 = jax.random.uniform(k_w2, (n_embd, d_ff), jnp.float32, -bound2, bound2)
        b2 = jax.random.uniform(k_b2, (n_embd,), jnp.float32, -bound2, bound2)
        return {'x': x, 'W1': W1, 'b1': b1, 'W2': W2, 'b2': b2}
    _L2_ffn_in = _L2_ffn_setup()

    def _L3_attn_setup():
        import jax, jax.numpy as jnp
        import numpy as np
        DIM = 128
        HEADS = 16
        DIM_HEAD = 64
        INNER = HEADS * DIM_HEAD
        N = 60
        B = 64
        NUM_FEATURES = 5
        NUM_REGIONS = 7
        REGIONS = [[1, 4, 10], [40, 47, 52], [2, 3, 5, 7, 8, 13], [44, 46, 49, 50, 51, 53], [6, 11, 14, 17, 18, 20, 25, 31, 32, 34, 39, 42, 45], [12, 24, 26, 38], [9, 15, 16, 19, 21, 22, 23, 27, 28, 29, 30, 33, 35, 36, 37, 41, 43, 48]]

        def build_interaction_mask(n):
            m = np.zeros((n, n), dtype=bool)
            for r, chans in enumerate(REGIONS):
                ch = [c + 6 for c in chans]
                m[r, ch] = True
                m[ch, r] = True
            m[:NUM_REGIONS, :NUM_REGIONS] = True
            m[NUM_REGIONS:, NUM_REGIONS:] = True
            return jnp.asarray(m)
        key = jax.random.key(seed)
        ks = jax.random.split(key, 9)
        s = 0.02
        return {'x': jax.random.normal(ks[0], (B, N, DIM), dtype=jnp.float32), 'ext_w1': jax.random.normal(ks[1], (NUM_FEATURES, DIM, DIM // 2), dtype=jnp.float32) * s, 'ext_b1': jnp.zeros((NUM_FEATURES, DIM // 2), dtype=jnp.float32), 'ext_w2': jax.random.normal(ks[2], (NUM_FEATURES, DIM // 2), dtype=jnp.float32) * s, 'ext_b2': jnp.zeros((NUM_FEATURES,), dtype=jnp.float32), 'qkv_w': jax.random.normal(ks[3], (DIM, 3 * INNER), dtype=jnp.float32) * s, 'out_w': jax.random.normal(ks[4], (INNER, DIM), dtype=jnp.float32) * s, 'out_b': jnp.zeros((DIM,), dtype=jnp.float32), 'faw': jnp.ones((HEADS, NUM_FEATURES), dtype=jnp.float32)}
    _L3_attn_in = _L3_attn_setup()

    def _L3_ffn_setup():
        import jax, jax.numpy as jnp
        import numpy as np

        def _binarize(w):
            alpha = jax.lax.stop_gradient(jnp.mean(jnp.abs(w), axis=1, keepdims=True))
            bw = alpha * jnp.sign(w)
            return w + jax.lax.stop_gradient(bw - w)
        key = jax.random.key(seed)
        k1, k2, k3, k4, k5 = jax.random.split(key, 5)
        D, H = (128, 512)
        x = jax.random.normal(k1, (64, 196, D), dtype=jnp.float32)
        w1 = jax.random.normal(k2, (H, D), dtype=jnp.float32) * 0.02
        b1 = jax.random.normal(k3, (H,), dtype=jnp.float32) * 0.02
        w2 = jax.random.normal(k4, (D, H), dtype=jnp.float32) * 0.02
        b2 = jax.random.normal(k5, (D,), dtype=jnp.float32) * 0.02
        return {'x': x, 'w1': w1, 'b1': b1, 'w2': w2, 'b2': b2}
    _L3_ffn_in = _L3_ffn_setup()
    _d = {'L0_attn_x': _L0_attn_in['x'], 'L0_attn_W_Q': _L0_attn_in['W_Q'], 'L0_attn_b_Q': _L0_attn_in['b_Q'], 'L0_attn_W_K': _L0_attn_in['W_K'], 'L0_attn_b_K': _L0_attn_in['b_K'], 'L0_attn_W_V': _L0_attn_in['W_V'], 'L0_attn_b_V': _L0_attn_in['b_V'], 'L0_attn_W_O': _L0_attn_in['W_O'], 'L0_attn_b_O': _L0_attn_in['b_O'], 'L0_ffn_wg': _L0_ffn_in['wg'], 'L0_ffn_W': _L0_ffn_in['W'], 'L0_ffn_b': _L0_ffn_in['b'], 'L1_attn_w_q': _L1_attn_in['w_q'], 'L1_attn_w_k': _L1_attn_in['w_k'], 'L1_attn_w_v': _L1_attn_in['w_v'], 'L1_attn_w_u': _L1_attn_in['w_u'], 'L1_attn_b_u': _L1_attn_in['b_u'], 'L1_ffn_W_r': _L1_ffn_in['W_r'], 'L1_ffn_W_k': _L1_ffn_in['W_k'], 'L1_ffn_W_v': _L1_ffn_in['W_v'], 'L1_ffn_mu_r': _L1_ffn_in['mu_r'], 'L1_ffn_mu_k': _L1_ffn_in['mu_k'], 'L2_attn_q_weight': _L2_attn_in['q_weight'], 'L2_attn_v_weight': _L2_attn_in['v_weight'], 'L2_attn_out_w': _L2_attn_in['out_w'], 'L2_attn_out_b': _L2_attn_in['out_b'], 'L2_ffn_W1': _L2_ffn_in['W1'], 'L2_ffn_b1': _L2_ffn_in['b1'], 'L2_ffn_W2': _L2_ffn_in['W2'], 'L2_ffn_b2': _L2_ffn_in['b2'], 'L3_attn_ext_w1': _L3_attn_in['ext_w1'], 'L3_attn_ext_b1': _L3_attn_in['ext_b1'], 'L3_attn_ext_w2': _L3_attn_in['ext_w2'], 'L3_attn_ext_b2': _L3_attn_in['ext_b2'], 'L3_attn_qkv_w': _L3_attn_in['qkv_w'], 'L3_attn_out_w': _L3_attn_in['out_w'], 'L3_attn_out_b': _L3_attn_in['out_b'], 'L3_attn_faw': _L3_attn_in['faw'], 'L3_ffn_w1': _L3_ffn_in['w1'], 'L3_ffn_b1': _L3_ffn_in['b1'], 'L3_ffn_w2': _L3_ffn_in['w2'], 'L3_ffn_b2': _L3_ffn_in['b2']}
    _x0 = _d['L0_attn_x']
    _d['L0_attn_x'] = jax.random.normal(jax.random.fold_in(jax.random.key(seed), 1), (1, 2048, 128), dtype=_x0.dtype)
    del _x0
    return _d

def reference(L0_attn_x, L0_attn_W_Q, L0_attn_b_Q, L0_attn_W_K, L0_attn_b_K, L0_attn_W_V, L0_attn_b_V, L0_attn_W_O, L0_attn_b_O, L0_ffn_wg, L0_ffn_W, L0_ffn_b, L1_attn_w_q, L1_attn_w_k, L1_attn_w_v, L1_attn_w_u, L1_attn_b_u, L1_ffn_W_r, L1_ffn_W_k, L1_ffn_W_v, L1_ffn_mu_r, L1_ffn_mu_k, L2_attn_q_weight, L2_attn_v_weight, L2_attn_out_w, L2_attn_out_b, L2_ffn_W1, L2_ffn_b1, L2_ffn_W2, L2_ffn_b2, L3_attn_ext_w1, L3_attn_ext_b1, L3_attn_ext_w2, L3_attn_ext_b2, L3_attn_qkv_w, L3_attn_out_w, L3_attn_out_b, L3_attn_faw, L3_ffn_w1, L3_ffn_b1, L3_ffn_w2, L3_ffn_b2):

    def _L0_attn_ref(x, W_Q, b_Q, W_K, b_K, W_V, b_V, W_O, b_O):
        import jax, jax.numpy as jnp
        import numpy as np
        B, T, D = (4, 256, 128)
        H, Dh = (16, 64)
        Q = jnp.einsum('btd,hkd->bthk', x, W_Q) + b_Q
        K = jnp.einsum('btd,hkd->bthk', x, W_K) + b_K
        V = jnp.einsum('btd,hkd->bthk', x, W_V) + b_V
        d_head = W_Q.shape[1]
        scores = jnp.einsum('bqhk,bshk->bhqs', Q, K) / jnp.sqrt(jnp.asarray(d_head, x.dtype))
        attn = jax.nn.softmax(scores, axis=-1)
        out_h = jnp.einsum('bhqs,bshk->bqhk', attn, V)
        return jnp.einsum('bqhk,hdk->bqd', out_h, W_O) + b_O

    def _L0_ffn_ref(x, wg, W, b):
        import jax, jax.numpy as jnp
        import numpy as np
        H = 128
        E = 8
        B, S = (4, 256)
        Bb, Ss, Hh = x.shape
        Ee = wg.shape[1]
        T = Bb * Ss
        C = T // Ee
        xt = x.reshape(T, Hh)
        logits = xt @ wg
        probs = jax.nn.softmax(logits, axis=-1)
        idx = jnp.argmax(probs, axis=-1)
        mask = jax.nn.one_hot(idx, Ee, dtype=xt.dtype)
        locations = jnp.cumsum(mask, axis=0) - mask
        mask = mask * (locations < C).astype(xt.dtype)
        gate = jnp.sum(probs * mask, axis=-1)
        loc_s = jnp.sum(locations * mask, axis=-1).astype(jnp.int32)
        loc_oh = jax.nn.one_hot(loc_s, C, dtype=xt.dtype)
        dispatch = mask[:, :, None] * loc_oh[:, None, :]
        combine = gate[:, None, None] * dispatch
        exp_in = jnp.einsum('tec,th->ech', dispatch, xt)
        exp_out = jnp.einsum('ech,efh->ecf', exp_in, W) + b[:, None, :]
        out = jnp.einsum('tec,ecf->tf', combine, exp_out)
        return out.reshape(Bb, Ss, Hh)

    def _L1_attn_ref(x, w_q, w_k, w_v, w_u, b_u):
        import jax, jax.numpy as jnp
        import numpy as np
        EMB, HEADS, HIDDEN = (128, 16, 64)
        BS, N = (2, 256)
        bs, n, emb = x.shape
        h, hd = (HEADS, HIDDEN)
        q = (x @ w_q).reshape(bs, n, h, hd)
        k = (x @ w_k).reshape(bs, n, h, hd)
        v = (x @ w_v).reshape(bs, n, h, hd)
        scale = 1.0 / jnp.sqrt(jnp.asarray(hd, dtype=x.dtype))
        q = q * scale
        k = k * scale
        dot = jnp.einsum('bqhd,bkhd->bhqk', q, k)
        causal = jnp.tril(jnp.ones((n, n), dtype=bool))
        dot = jnp.where(causal, dot, jnp.asarray(-jnp.inf, dtype=dot.dtype))
        att = jax.nn.softmax(dot, axis=-1)
        out = jnp.einsum('bhqk,bkhd->bqhd', att, v).reshape(bs, n, h * hd)
        return out @ w_u + b_u

    def _L1_ffn_ref(x, W_r, W_k, W_v, mu_r, mu_k):
        import jax, jax.numpy as jnp
        import numpy as np
        DIM = 128

        def _reference_tuple_inner(x, W_r, W_k, W_v, mu_r, mu_k):
            B, T, C = x.shape
            x_prev = jnp.concatenate([jnp.zeros((B, 1, C), x.dtype), x[:, :-1, :]], axis=1)
            xr = mu_r * x + (1.0 - mu_r) * x_prev
            xk = mu_k * x + (1.0 - mu_k) * x_prev
            r = jax.nn.sigmoid(jnp.einsum('btc,dc->btd', xr, W_r))
            k = jnp.einsum('btc,dc->btd', xk, W_k)
            k_act = jnp.square(jax.nn.relu(k))
            out = r * jnp.einsum('btc,dc->btd', k_act, W_v)
            new_state = x[:, -1, :]
            return (out, new_state)
        return _reference_tuple_inner(x, W_r, W_k, W_v, mu_r, mu_k)[0]

    def _L2_attn_ref(x, q_weight, v_weight, out_w, out_b):
        import jax, jax.numpy as jnp
        import numpy as np
        import math
        T, N, D, H = (256, 2, 128, 16)
        HD = D // H
        head_dim = q_weight.shape[-1]
        inv_sqrt_d = 1.0 / math.sqrt(head_dim)
        q = jnp.einsum('tbm,mhd->tbhd', x, q_weight)
        q_sq = jnp.einsum('tbhd,tbhd->tbh', q, q)
        squared_dist = q_sq[:, None] + q_sq[None, :] - 2.0 * jnp.einsum('tbhd,sbhd->tsbh', q, q)
        attn_logits = -squared_dist * inv_sqrt_d
        attn_weights = jax.nn.softmax(attn_logits, axis=1)
        A = jnp.einsum('mhd,nhd->hmn', q_weight, q_weight) * inv_sqrt_d
        XA = jnp.einsum('tbm,hmn->tbhn', x, A)
        PXA = jnp.einsum('tsbh,sbhm->tbhm', attn_weights, XA)
        PXAV = jnp.einsum('tbhm,mhd->tbhd', PXA, v_weight).reshape(x.shape[0], x.shape[1], -1)
        return PXAV @ out_w.T + out_b

    def _L2_ffn_ref(x, W1, b1, W2, b2):
        import jax, jax.numpy as jnp
        import numpy as np
        EPS = 1e-05

        def _quantize(W):
            gamma = jnp.mean(jnp.abs(W))
            return jnp.clip(jnp.round(W / (gamma + EPS)), -1.0, 1.0)
        Wq1 = _quantize(W1)
        Wq2 = _quantize(W2)
        h = jax.nn.relu(jnp.einsum('bsd,fd->bsf', x, Wq1) + b1)
        out = jnp.einsum('bsf,df->bsd', h, Wq2) + b2
        return out

    def _L3_attn_ref(x, ext_w1, ext_b1, ext_w2, ext_b2, qkv_w, out_w, out_b, faw):
        import jax, jax.numpy as jnp
        import numpy as np
        DIM = 128
        HEADS = 16
        DIM_HEAD = 64
        INNER = HEADS * DIM_HEAD
        N = 60
        B = 64
        NUM_FEATURES = 5
        NUM_REGIONS = 7
        REGIONS = [[1, 4, 10], [40, 47, 52], [2, 3, 5, 7, 8, 13], [44, 46, 49, 50, 51, 53], [6, 11, 14, 17, 18, 20, 25, 31, 32, 34, 39, 42, 45], [12, 24, 26, 38], [9, 15, 16, 19, 21, 22, 23, 27, 28, 29, 30, 33, 35, 36, 37, 41, 43, 48]]

        def build_interaction_mask(n):
            m = np.zeros((n, n), dtype=bool)
            for r, chans in enumerate(REGIONS):
                ch = [c + 6 for c in chans]
                m[r, ch] = True
                m[ch, r] = True
            m[:NUM_REGIONS, :NUM_REGIONS] = True
            m[NUM_REGIONS:, NUM_REGIONS:] = True
            return jnp.asarray(m)
        b, n, d = x.shape
        scale = DIM_HEAD ** (-0.5)
        hmid = jax.nn.gelu(jnp.einsum('bnd,fdk->bfnk', x, ext_w1) + ext_b1[None, :, None, :], approximate=False)
        feature_scores = jax.nn.sigmoid(jnp.einsum('bfnk,fk->bfn', hmid, ext_w2) + ext_b2[None, :, None]).transpose(0, 2, 1)
        qkv = x @ qkv_w
        q, k, v = jnp.split(qkv, 3, axis=-1)
        to_heads = lambda t: t.reshape(b, n, HEADS, DIM_HEAD).transpose(0, 2, 1, 3)
        q, k, v = (to_heads(q), to_heads(k), to_heads(v))
        dots = jnp.einsum('bhid,bhjd->bhij', q, k) * scale
        mask = build_interaction_mask(n)
        neg = -jnp.finfo(dots.dtype).max
        dots = jnp.where(mask[None, None, :, :], dots, neg)
        fw = jax.nn.softmax(faw, axis=-1)
        bias = jnp.einsum('bnf,hf->bhn', feature_scores, fw)[..., None]
        attn = jax.nn.softmax(dots + bias, axis=-1)
        out = jnp.einsum('bhij,bhjd->bhid', attn, v)
        out = out.transpose(0, 2, 1, 3).reshape(b, n, INNER)
        return out @ out_w + out_b

    def _L3_ffn_ref(x, w1, b1, w2, b2):
        import jax, jax.numpy as jnp
        import numpy as np

        def _binarize(w):
            alpha = jax.lax.stop_gradient(jnp.mean(jnp.abs(w), axis=1, keepdims=True))
            bw = alpha * jnp.sign(w)
            return w + jax.lax.stop_gradient(bw - w)
        bw1 = _binarize(w1)
        h = jnp.einsum('bsd,hd->bsh', x, bw1) + b1
        h = jax.nn.gelu(h, approximate=False)
        bw2 = _binarize(w2)
        out = jnp.einsum('bsh,dh->bsd', h, bw2) + b2
        return out
    x = L0_attn_x
    x = x + _L0_attn_ref(_layernorm(x, axis=-1), L0_attn_W_Q, L0_attn_b_Q, L0_attn_W_K, L0_attn_b_K, L0_attn_W_V, L0_attn_b_V, L0_attn_W_O, L0_attn_b_O)
    x = x + _L0_ffn_ref(_layernorm(x, axis=-1), L0_ffn_wg, L0_ffn_W, L0_ffn_b)
    x = x + _L1_attn_ref(_layernorm(x, axis=-1), L1_attn_w_q, L1_attn_w_k, L1_attn_w_v, L1_attn_w_u, L1_attn_b_u)
    x = x + _L1_ffn_ref(_layernorm(x, axis=-1), L1_ffn_W_r, L1_ffn_W_k, L1_ffn_W_v, L1_ffn_mu_r, L1_ffn_mu_k)
    x = x + _L2_attn_ref(_layernorm(x, axis=-1), L2_attn_q_weight, L2_attn_v_weight, L2_attn_out_w, L2_attn_out_b)
    x = x + _L2_ffn_ref(_layernorm(x, axis=-1), L2_ffn_W1, L2_ffn_b1, L2_ffn_W2, L2_ffn_b2)
    x = x + _L3_attn_ref(_layernorm(x, axis=-1), L3_attn_ext_w1, L3_attn_ext_b1, L3_attn_ext_w2, L3_attn_ext_b2, L3_attn_qkv_w, L3_attn_out_w, L3_attn_out_b, L3_attn_faw)
    x = x + _L3_ffn_ref(_layernorm(x, axis=-1), L3_ffn_w1, L3_ffn_b1, L3_ffn_w2, L3_ffn_b2)
    return x

_drawn_inputs = setup_inputs


def setup_inputs(seed=0):
    import zlib

    import numpy as np

    out = dict(_drawn_inputs(seed))
    spreads = {'L0_attn_b_Q': (0.0, 0.8),
     'L0_attn_b_K': (0.0, 2.0),
     'L0_attn_b_V': (0.0, 0.1),
     'L0_attn_b_O': (0.0, 0.1),
     'L3_attn_ext_b1': (0.0, 2.0),
     'L3_attn_ext_b2': (0.0, 2.0),
     'L3_attn_out_b': (0.0, 2.0),
     'L3_attn_faw': (1.0, 0.6)}
    factors = {'L0_attn_W_Q': 8.0,
     'L0_attn_W_K': 8.0,
     'L0_attn_W_V': 8.0,
     'L0_ffn_b': 8.0,
     'L1_attn_w_q': 8.0,
     'L1_attn_w_k': 8.0,
     'L1_attn_b_u': 2.756,
     'L1_ffn_W_r': 3.181,
     'L1_ffn_mu_r': 6.314,
     'L2_attn_q_weight': 8.0,
     'L2_attn_v_weight': 8.0,
     'L2_attn_out_w': 8.0,
     'L2_attn_out_b': 2.887,
     'L2_ffn_b1': 8.0,
     'L2_ffn_b2': 200.0,
     'L3_attn_ext_w1': 200.0,
     'L3_attn_ext_w2': 200.0,
     'L3_attn_qkv_w': 8.0,
     'L3_attn_out_w': 8.0,
     'L3_ffn_w1': 25.915,
     'L3_ffn_b1': 64.0,
     'L3_ffn_w2': 23.147,
     'L3_ffn_b2': 200.0}
    for name, (base, spread) in spreads.items():
        noise = np.random.default_rng([zlib.crc32(name.encode()), seed]).standard_normal(out[name].shape)
        drawn = base * np.exp(spread * noise) if base else spread * noise
        out[name] = jnp.asarray(drawn.astype(out[name].dtype))
    for name, factor in factors.items():
        out[name] = (out[name] * factor).astype(out[name].dtype)
    return out
```

```python
from contextlib import ExitStack

import numpy as np

import concourse.bass as bass
from concourse import mybir

F32 = mybir.dt.float32
F32R = mybir.dt.float32r
BF16 = mybir.dt.bfloat16
ALU = mybir.AluOpType
ACT = mybir.ActivationFunctionType
AX = mybir.AxisListType

P = 128
T = 2048
D = 128
NT = T // P
CH = 512
NC = T // CH
TPC = CH // P
HEADS, DH = 16, 64
PAIRS = HEADS // 2
E_EXP = 8
CAP = T // E_EXP
FF = 512
NJ = FF // P
EPS = 1e-5
BIG = 2.0 ** 100
LOWEST = -3.0e38
NREG = 7
REGIONS = [[1, 4, 10], [40, 47, 52], [2, 3, 5, 7, 8, 13], [44, 46, 49, 50, 51, 53],
           [6, 11, 14, 17, 18, 20, 25, 31, 32, 34, 39, 42, 45], [12, 24, 26, 38],
           [9, 15, 16, 19, 21, 22, 23, 27, 28, 29, 30, 33, 35, 36, 37, 41, 43, 48]]
NF, FH = 5, 64
ROW_M, ROW_B, ROW_R, ROW_C = 64, 65, 66, 73

SLOTS = 16
LAG = 2


def causal_tiles():
    return [(c, j, max(0, j - TPC * c) * P) for c in range(NC) for j in range(TPC * (c + 1))]


def full_tiles():
    return [(c, j, 0) for c in range(NC) for j in range(NT)]


class Layer:

    def __init__(self, n, causal, scale, biased, featured):
        self.n, self.causal, self.scale = n, causal, scale
        self.biased, self.featured = biased, featured
        self.tiles = causal_tiles() if causal else full_tiles()
        self.G = len(self.tiles)
        self.end = [max(g for g, t in enumerate(self.tiles) if t[0] == c) + 1 for c in range(NC)]
        self.loads = 3 + (3 if biased else 0)

    def keys(self, t):
        return (t + 1) * P if self.causal else T


LAYERS = [Layer(0, False, 0.125, True, False), Layer(1, True, 1.0 / 64, False, False),
          Layer(2, False, 0.125, False, True)]


def program(nc, a, out):
    with ExitStack() as ctx:
        def sb(name, shape, dt=F32):
            return ctx.enter_context(nc.sbuf_tensor(name, shape, dt))

        def sem(name):
            return ctx.enter_context(nc.semaphore(name))

        x = sb("x", [P, NT, D])
        yT = sb("yT", [P, T + 2])
        S1 = [sb(f"S1_{h}", [P, T], F32R) for h in range(2)]
        M1 = [sb(f"M1_{h}", [P, T], F32R) for h in range(2)]
        S2 = [sb(f"S2_{h}", [P, T], F32R) for h in range(2)]
        M2 = [sb(f"M2_{h}", [P, T], F32R) for h in range(2)]
        V = sb("V", [P, NT, P])
        work = sb("work", [P, SLOTS, CH])
        acc = sb("acc", [P, 2, 2, CH])
        smax = sb("smax", [P, 2, T // 2])
        scan = sb("scan", [P, 2, T // 2])
        mcol = sb("mcol", [P, 2 * NT])
        mT = sb("mT", [2 * NT, P], F32R)
        oT = sb("oT", [P, 2, CH])
        rinv = sb("rinv", [P, CH])
        wqkv = sb("wqkv", [P, 3, P])
        wo = sb("wo", [P, P])
        bqk = sb("bqk", [P, 2])
        bv = sb("bv", [P, P])
        zrow = sb("zrow", [1, 1, CH])
        zcol = sb("zcol", [P, 1])
        ident = sb("ident", [P, P])
        identb = sb("identb", [P, P], BF16)
        maskqs = sb("maskqs", [P, P])
        masksq = sb("masksq", [P, P])
        maskqsb = sb("maskqsb", [P, P], BF16)
        masksqb = sb("masksqb", [P, P], BF16)
        before = sb("before", [P, P])
        ones = sb("ones", [P, P])
        obias = sb("obias", [P, 6, D])
        stats = sb("stats", [P, NT, 6])
        mv = sb("mv", [P, NT, 2])
        sd = sb("sd", [P, NT])
        rstd = sb("rstd", [P, NT])
        wg = sb("wg", [P, E_EXP])
        wexp = sb("wexp", [P, E_EXP, D])
        bexp = sb("bexp", [E_EXP, D])
        first = sb("first", [P, E_EXP])
        small = sb("small", [P, 8, NT, E_EXP])
        few = sb("few", [P, 4, NT])
        coefT = sb("coefT", [E_EXP, 2, P])
        wmix = sb("wmix", [P, 3, D])
        mu = sb("mu", [P, 4])
        wl2 = sb("wl2", [P, 5, D])
        l2 = sb("l2", [P, 3, D])
        wt = sb("wt", [P, 4, FF])
        wm = sb("wm", [P, 4, FF])
        wtmp = sb("wtmp", [P, FF])
        b1 = sb("b1", [P, 2, NJ])
        gam = sb("gam", [P, 8])
        wext = sb("wext", [P, NF * FH])
        bext = sb("bext", [P, 3])
        w2ext = sb("w2ext", [P, 3])
        w2m = sb("w2m", [P, 3, NF])
        w2b = sb("w2b", [P, 3, NF])
        b2ext = sb("b2ext", [NF, 1])
        faw = sb("faw", [HEADS, 8])
        fawT = sb("fawT", [NF, HEADS])
        fs = sb("fs", [NF, CH])
        brow = sb("brow", [HEADS, CH])
        brow_dram = nc.dram_tensor("bias_rows", [HEADS, T], F32, kind="Internal").ap()

        ps = ctx.enter_context(nc.psum_tensor("ps", [P, 8, CH], F32))

        def bank(b):
            return ps[:, b, :]

        yv = yT[:, 1:T + 1]

        const_in = sem("const_in")
        x_in = sem("x_in")
        dve_step = sem("dve_step")
        consts_ready = sem("consts_ready")
        var_ready = sem("var_ready")
        sd_ready = sem("sd_ready")
        yn_ready = sem("yn_ready")
        yt_psum = sem("yt_psum")
        yt_ready = sem("yt_ready")
        out_done = sem("out_done")

        A = [{k: sem(f"{k}_{L.n}") for k in (
            "w_loaded",
            "wo_loaded",
            "zero_done",
            "proj_ready",
            "hi_ready",
            "lo_ready",
            "dup_done",
            "sc_ready",
            "cp_ready",
            "scan_ready",
            "mcol_ready",
            "mt_psum",
            "mt_ready",
            "mrow_done",
            "v_psum",
            "v_ready",
            "st_ready",
            "p_ready",
            "acc_ready",
            "pv_done",
            "den_ready",
            "rinv_ready",
            "ot_ready",
            "op_ready",
            "x_added",
        )} for L in LAYERS]
        aux_ready = sem("aux_ready")
        aux_in = sem("aux_in")
        row_ready = sem("row_ready")
        fw_in, fw_exp = sem("fw_in"), sem("fw_exp")
        lg_ready, dl_ready, ex_ready, mask_ready, loc_psum, cf_ready = (
            sem(s) for s in ("lg_ready", "dl_ready", "ex_ready", "mask_ready", "loc_psum", "cf_ready"))
        cT_psum, cT_ready, xp_psum, xp_used, x_exp = (
            sem(s) for s in ("cT_psum", "cT_ready", "xp_psum", "xp_used", "x_exp"))
        mix_ready, r_psum, r_ready, k_psum, kr_ready, k_ready, mo_psum, mo_used = (
            sem(s) for s in ("mix_ready", "r_psum", "r_ready", "k_psum", "kr_ready", "k_ready",
                             "mo_psum", "mo_used"))
        l2_psum, l2_ready, lo_psum, lo_used = (
            sem(s) for s in ("l2_psum", "l2_ready", "lo_psum", "lo_used"))
        gam_in, gam_psum, wm_ready, wT_psum, wT_ready = (
            sem(s) for s in ("gam_in", "gam_psum", "wm_ready", "wT_psum", "wT_ready"))
        F = [{k: sem(f"{k}_{n}") for k in ("h_psum", "h_ready", "f_psum", "f_used")} for n in range(2)]
        ft_psum, ft_ready, fw_ready, fwT_psum, fwT_ready, br_psum, br_ready, br_out = (
            sem(s) for s in ("ft_psum", "ft_ready", "fw_ready", "fwT_psum", "fwT_ready", "br_psum",
                             "br_ready", "br_out"))

        block = ctx.enter_context(nc.Block())

        wcols = [("L0_wq", "L0_wk", "L0_wv"), ("L1_attn_w_q", "L1_attn_w_k", "L1_attn_w_v"), None]
        wouts = ["L0_wo", "L1_attn_w_u", "L3_attn_out_w"]

        def rows(ap, n=P):
            return ap.rearrange("(o d) -> o d", o=1).to_broadcast([n, ap.shape[0]])

        def column(ap):
            return ap.rearrange("(p o) -> p o", o=1)

        const_loads = [
            (ident[:], a["c_ident"]), (maskqs[:], a["c_maskqs"]), (masksq[:], a["c_masksq"]),
            (wt[:], a["mlp_w"]), (b1[:], a["mlp_b1"]),
            (before[:], a["c_before"]), (first[:], a["c_first"]), (wl2[:, 4, :], a["c_block"]),
            (wg[:], a["L0_ffn_wg"]), (wexp[:], a["L0_wexp"]), (bexp[:], a["L0_ffn_b"]),
            (wmix[:], a["L1_wmix"]), (mu[:, 0:1], column(a["L1_ffn_mu_r"])), (mu[:, 1:2], column(a["L1_ffn_mu_k"])),
            (wl2[:, 0:4, :], a["L2_w"]),
            (wext[:], a["L3_wext"]), (bext[:], a["L3_bext"]), (w2ext[:], a["L3_w2ext"]), (w2m[:], a["c_w2m"]),
            (b2ext[:], column(a["L3_attn_ext_b2"])), (faw[:, 0:NF], a["L3_attn_faw"]),
        ] + [(obias[:, n, :], rows(a[k])) for n, k in enumerate(
            ("L0_attn_b_O", "L1_attn_b_u", "L2_attn_out_b", "L2_ffn_b2", "L3_attn_out_b", "L3_ffn_b2"))]
        N_CONST = len(const_loads)

        @block.sync
        def _(sp):
            sp.dma_start(x[:], a["L0_attn_x"].rearrange("b (t p) d -> p (b t) d", p=P)).then_inc(x_in, 16)
            for dst, src in const_loads:
                sp.dma_start(dst, src).then_inc(const_in, 16)

            sp.wait_ge(consts_ready, 1)
            for L in LAYERS:
                s = A[L.n]
                if L.n:
                    sp.wait_ge(A[L.n - 1]["v_ready"], PAIRS * NC + 1)
                    sp.wait_ge(A[L.n - 1]["op_ready"], PAIRS * NC + 1)
                if L.featured:
                    for c in range(NC):
                        sp.wait_ge(br_ready, c + 1)
                        sp.dma_start(brow_dram[:, c * CH:(c + 1) * CH], brow[:]).then_inc(br_out, 16)
                        sp.wait_ge(br_out, 16 * (c + 1))
                    sp.dma_start(V[:].rearrange("p t d -> p (t d)"), a["c_aux"]).then_inc(aux_in, 16)
                    sp.wait_ge(aux_ready, 2)
                sp.sem_inc(s["v_ready"], 1)
                sp.sem_inc(s["op_ready"], 1)
                with sp.Fori(0, PAIRS) as i:
                    sp.wait_ge(s["v_ready"], i * NC + 1)
                    for n in range(3):
                        if wcols[L.n]:
                            src = a[wcols[L.n][n]][:, bass.ds(i * P, P)]
                        else:
                            src = a["L3_attn_qkv_w"][:, n * HEADS * DH:(n + 1) * HEADS * DH][:, bass.ds(i * P, P)]
                        sp.dma_start(wqkv[:, n, :], src).then_inc(s["w_loaded"], 16)
                    if L.biased:
                        sp.dma_start(bqk[:, 0:1], a["L0_bq"][bass.ds(i * P, P), :]).then_inc(s["w_loaded"], 16)
                        sp.dma_start(bqk[:, 1:2], a["L0_bk"][bass.ds(i * P, P), :]).then_inc(s["w_loaded"], 16)
                        sp.dma_start(bv[:], a["L0_bv"][:, bass.ds(i * P, P)].to_broadcast([P, P])).then_inc(s["w_loaded"], 16)
                    sp.wait_ge(s["op_ready"], i * NC + 1)
                    sp.dma_start(wo[:], a[wouts[L.n]][bass.ds(i * P, P), :]).then_inc(s["wo_loaded"], 16)
                    for h in range(2):
                        sp.dma_start(M1[h][ROW_M:ROW_M + 1, :].bitcast(F32).rearrange("o (c q) -> o c q", c=NC),
                                     zrow[:].to_broadcast([1, NC, CH])).then_inc(s["zero_done"], 16)
                        if L.featured:
                            sp.dma_start(M1[h][ROW_B:ROW_B + 1, :].bitcast(F32),
                                         brow_dram[bass.ds(i * 2 + h, 1), :]).then_inc(s["zero_done"], 16)
                    sp.wait_ge(s["hi_ready"], i * 16 + 16)
                    for h in range(2):
                        sp.dma_start(M2[h][DH:P, :].bitcast(F32), M1[h][0:DH, :].bitcast(F32)).then_inc(s["dup_done"], 16)
                        sp.dma_start(S2[h][0:DH, :].bitcast(F32), S1[h][0:DH, :].bitcast(F32)).then_inc(s["dup_done"], 16)
                    sp.wait_ge(s["mt_ready"], i + 1)
                    for h in range(2):
                        sp.dma_start(M1[h][ROW_M:ROW_M + 1, :].bitcast(F32).rearrange("o (t p) -> o t p", p=P),
                                     mT[h * NT:(h + 1) * NT, :].bitcast(F32)).then_inc(s["mrow_done"], 16)
            sp.wait_ge(F[1]["f_used"], NC)
            sp.dma_start(out.rearrange("b (t p) d -> p (b t) d", p=P), x[:]).then_inc(out_done, 16)
            sp.wait_ge(out_done, 16)

        @block.tensor
        def _(pe):
            def layernorm(k):
                for t in range(NT):
                    pe.wait_ge(yn_ready, k * NT + t + 1)
                    mm = pe.transpose(ps[:, t // TPC, (t % TPC) * P:(t % TPC + 1) * P],
                                      work[:, t // TPC, (t % TPC) * P:(t % TPC + 1) * P], ident[:])
                    if t % TPC == TPC - 1:
                        mm.then_inc(yt_psum, 1)

            def attention(L):
                s = A[L.n]
                with pe.Fori(0, PAIRS) as i:
                    pe.wait_ge(s["w_loaded"], i * (16 * L.loads) + 16 * L.loads)
                    for n in range(2 * NC):
                        c, qk = n // 2, n % 2
                        if n >= 4:
                            pe.wait_ge(s["lo_ready"], i * 16 + 2 * (n - 4) + 2)
                            pe.wait_ge(s["hi_ready"], i * 16 + 2 * (n - 4) + 2)
                        pe.matmul(bank(n % 4), wqkv[:, qk, :], yv[:, c * CH:(c + 1) * CH],
                                  start=True, stop=True).then_inc(s["proj_ready"], 1)
                    pe.wait_ge(s["zero_done"], i * (64 if L.featured else 32) + (64 if L.featured else 32))
                    pe.wait_ge(s["hi_ready"], i * 16 + 16)
                    pe.wait_ge(s["lo_ready"], i * 16 + 16)
                    for n in range(2 * NT):
                        h, t = n // NT, n % NT
                        if n >= 2:
                            pe.wait_ge(s["scan_ready"], i * 2 * NT + n - 1)
                        g4 = 4 * (n % 2)
                        w = L.keys(t)
                        for j in range((w + CH - 1) // CH):
                            cols = min(CH, w - j * CH)
                            last = j == (w + CH - 1) // CH - 1
                            mm = pe.matmul(ps[:, g4 + j, 0:cols], M1[h][:, t * P:(t + 1) * P],
                                           S1[h][:, j * CH:j * CH + cols], start=True,
                                           stop=not (L.causal and last))
                            if L.causal and last:
                                mm = pe.matmul(ps[:, g4 + j, cols - P:cols], identb[:], maskqsb[:],
                                               start=False, stop=True)
                        mm.then_inc(s["sc_ready"], 1)
                    pe.wait_ge(s["scan_ready"], i * 2 * NT + 2 * NT)
                    pe.wait_ge(s["mcol_ready"], i * 2 * NT + 2 * NT)
                    pe.transpose(ps[0:2 * NT, 0, 0:P], mcol[:], ident[:]).then_inc(s["mt_psum"], 1)
                    for c in range(NC):
                        for t in range(TPC):
                            mm = pe.matmul(ps[:, 4 + c, t * P:(t + 1) * P],
                                           yv[:, (c * TPC + t) * P:(c * TPC + t + 1) * P],
                                           wqkv[:, 2, :], start=True, stop=True)
                        mm.then_inc(s["v_psum"], 1)

                    def values(g):
                        c, j, q0 = L.tiles[g]
                        if j == 0 and c >= 2:
                            pe.wait_ge(s["ot_ready"], i * NC + c - 1)
                        pe.wait_ge(s["p_ready"], i * (2 * L.G) + 2 * g + 2)
                        last = g + 1 == L.end[c]
                        for h in range(2):
                            mm = pe.matmul(ps[h * DH:(h + 1) * DH, 4 + c % 2, q0:CH],
                                           V[:, j, h * DH:(h + 1) * DH], work[:, (2 * g + h) % SLOTS, q0:CH],
                                           start=(j == 0), stop=last, skip_group_check=True)
                        mm.then_inc(s["pv_done"], 1)

                    def denominators(c):
                        pe.wait_ge(s["acc_ready"], i * (2 * L.G) + 2 * L.end[c])
                        if c >= 1:
                            pe.wait_ge(s["rinv_ready"], i * NC + c)
                        for h in range(2):
                            mm = pe.matmul(ps[h * DH:(h + 1) * DH, 6, :], ones[:, 0:DH], acc[:, c % 2, h, :],
                                           start=True, stop=True, skip_group_check=True)
                        mm.then_inc(s["den_ready"], 1)

                    def project_out(c):
                        if c == 0:
                            pe.wait_ge(s["wo_loaded"], i * 16 + 16)
                        else:
                            pe.wait_ge(s["x_added"], i * NC + c)
                        pe.wait_ge(s["ot_ready"], i * NC + c + 1)
                        for t in range(TPC):
                            mm = pe.matmul(ps[:, 7, t * P:(t + 1) * P], oT[:, c % 2, t * P:(t + 1) * P], wo[:],
                                           start=True, stop=True)
                        mm.then_inc(s["op_ready"], 1)

                    pe.wait_ge(s["mrow_done"], i * 32 + 32)
                    pe.wait_ge(s["dup_done"], i * 64 + 64)
                    pe.wait_ge(s["v_ready"], i * NC + NC + 1)
                    for g in range(L.G + LAG):
                        if g < L.G:
                            c, j, q0 = L.tiles[g]
                            diagonal = L.causal and j >= TPC * c
                            for h in range(2):
                                if g >= 2:
                                    pe.wait_ge(s["p_ready"], i * (2 * L.G) + 2 * (g - 2) + h + 1)
                                o = ps[:, (2 * g + h) % 4, q0:CH]
                                pe.matmul(o, S1[h][:, j * P:(j + 1) * P], M1[h][:, c * CH + q0:(c + 1) * CH],
                                          start=True, stop=False)
                                mm = pe.matmul(o, S2[h][:, j * P:(j + 1) * P], M2[h][:, c * CH + q0:(c + 1) * CH],
                                               start=False, stop=not diagonal)
                                if diagonal:
                                    mm = pe.matmul(ps[:, (2 * g + h) % 4, q0:q0 + P], identb[:], masksqb[:],
                                                   start=False, stop=True)
                                mm.then_inc(s["st_ready"], 1)
                        if g >= LAG:
                            values(g - LAG)
                        for c in range(NC):
                            if g == L.end[c] + LAG + 1 and c < NC - 1:
                                denominators(c)
                            if g == L.end[c] + LAG + 4 and c < NC - 1:
                                project_out(c)
                    if L.end[NC - 2] + LAG + 4 >= L.G + LAG:
                        raise AssertionError("the last chunk is too short")
                    denominators(NC - 1)
                    project_out(NC - 1)

            def experts():
                pe.wait_ge(yt_ready, 2 * NC)
                pe.wait_ge(const_in, 16 * N_CONST)
                for t in range(NT):
                    mm = pe.matmul(ps[:, 0, t * E_EXP:(t + 1) * E_EXP], yv[:, t * P:(t + 1) * P], wg[:],
                                   start=True, stop=True)
                mm.then_inc(lg_ready, 1)
                pe.wait_ge(mask_ready, 1)
                m = small[:, 4, :, :].rearrange("p t e -> p (t e)")
                pe.matmul(ps[:, 1, 0:P], before[:], m, start=True, stop=True)
                pe.matmul(ps[:, 2, 0:P], ones[:], m, start=True, stop=True).then_inc(loc_psum, 1)
                pe.wait_ge(cf_ready, 1)
                for t in range(NT):
                    pe.transpose(ps[0:E_EXP, 3 + t % 2, 0:P], small[:, 5, t, :], ident[:]).then_inc(cT_psum, 1)
                    if t >= 1:
                        expert_tile(t - 1)
                expert_tile(NT - 1)

            def expert_tile(t):
                if t >= 2:
                    pe.wait_ge(x_exp, E_EXP * (t - 2) + E_EXP)
                b0 = 6 if t % 2 == 0 else 0
                for k in range(2):
                    pe.matmul(bank(b0 + k), yv[:, t * P:(t + 1) * P],
                              wexp[:, 4 * k:4 * k + 4, :].rearrange("p e f -> p (e f)"), start=True, stop=True)
                pe.wait_ge(cT_ready, t + 1)
                pe.matmul(ps[:, 5 if t % 2 == 0 else 2, 0:D], coefT[:, t % 2, :], bexp[:], start=True, stop=True).then_inc(xp_psum, 1)

            def channel_mix():
                for c in range(NC):
                    pe.wait_ge(mix_ready, 2 * c + 2)
                    if c >= 2:
                        pe.wait_ge(r_ready, c - 1)
                        pe.wait_ge(kr_ready, c - 1)
                    for t in range(TPC):
                        mm = pe.matmul(ps[:, c % 2, t * P:(t + 1) * P],
                                       work[:, c, t * P:(t + 1) * P], wmix[:, 0, :],
                                       start=True, stop=True)
                    mm.then_inc(r_psum, 1)
                    pe.matmul(bank(2 + c % 2), wmix[:, 1, :], work[:, 4 + c, :], start=True, stop=True).then_inc(k_psum, 1)
                    if c >= 1:
                        mix_out(c - 1)
                mix_out(NC - 1)

            def mix_out(c):
                pe.wait_ge(k_ready, c + 1)
                for t in range(TPC):
                    mm = pe.matmul(ps[:, 4 + c, t * P:(t + 1) * P], work[:, 4 + c, t * P:(t + 1) * P], wmix[:, 2, :],
                                   start=True, stop=True)
                mm.then_inc(mo_psum, 1)

            def l2_attention():
                pe.matmul(ps[:, 4, 0:D], wl2[:, 0, :], wl2[:, 1, :], start=True, stop=True).then_inc(l2_psum, 1)
                pe.wait_ge(l2_ready, 1)
                pe.matmul(ps[:, 5, 0:D], l2[:, 0, :], wl2[:, 2, :], start=True, stop=True).then_inc(l2_psum, 1)
                pe.wait_ge(l2_ready, 2)
                pe.matmul(ps[:, 6, 0:D], l2[:, 1, :], wl2[:, 3, :], start=True, stop=True).then_inc(l2_psum, 1)
                pe.wait_ge(l2_ready, 3)
                for c in range(NC):
                    pe.wait_ge(yt_ready, 4 * NC + c + 1)
                    for t in range(TPC):
                        mm = pe.matmul(ps[:, c, t * P:(t + 1) * P], yv[:, (c * TPC + t) * P:(c * TPC + t + 1) * P],
                                       l2[:, 2, :], start=True, stop=True)
                    mm.then_inc(lo_psum, 1)

            def mlp(n, k):
                s = F[n]
                for c in range(NC):
                    pe.wait_ge(yt_ready, k * NC + c + 1)
                    for j in range(NJ):
                        m = c * NJ + j
                        if m >= 4:
                            pe.wait_ge(s["h_ready"], m - 3)
                        else:
                            pe.wait_ge(yt_ready, k * NC + m + 1)
                        pe.matmul(bank(m % 4), wm[:, 2 * n, j * P:(j + 1) * P], yv[:, c * CH:(c + 1) * CH],
                                  start=True, stop=True).then_inc(s["h_psum"], 1)
                    if c >= 1:
                        mlp_out(n, c - 1)
                mlp_out(n, NC - 1)

            def mlp_out(n, c):
                s = F[n]
                pe.wait_ge(s["h_ready"], NJ * (c + 1))
                for t in range(TPC):
                    for j in range(NJ):
                        mm = pe.matmul(ps[:, 4 + c, t * P:(t + 1) * P], work[:, j * 4 + c, t * P:(t + 1) * P],
                                       wm[:, 2 * n + 1, j * P:(j + 1) * P], start=(j == 0), stop=(j == NJ - 1))
                mm.then_inc(s["f_psum"], 1)

            def weights():
                pe.wait_ge(gam_in, 1)
                pe.matmul(ps[:, 0, 0:2], ones[:], gam[:, 0:2], start=True, stop=True).then_inc(gam_psum, 1)
                pe.wait_ge(wm_ready, 2)
                for m in range(2):
                    for j in range(NJ):
                        mm = pe.transpose(ps[:, 1 + m, j * P:(j + 1) * P], work[:, 4 + m, j * P:(j + 1) * P], ident[:])
                    mm.then_inc(wT_psum, 1)

            def features():
                pe.wait_ge(fw_ready, 1)
                pe.transpose(ps[0:NF, 7, 0:HEADS], faw[:, 0:NF], ident[0:HEADS, 0:HEADS]).then_inc(fwT_psum, 1)
                pe.wait_ge(yt_ready, 7 * NC)
                for c in range(NC):
                    for m in range(3):
                        M = P if m < 2 else FH
                        if c >= 1:
                            pe.wait_ge(ft_ready, 4 * (c - 1) + m + 1)
                        pe.matmul(ps[0:M, m, :], wext[:, m * P:m * P + M], yv[:, c * CH:(c + 1) * CH],
                                  start=True, stop=True).then_inc(ft_psum, 1)
                    pe.wait_ge(ft_ready, 4 * c + 3)
                    for m in range(3):
                        M = P if m < 2 else FH
                        mm = pe.matmul(ps[0:NF, 3, :], w2b[0:M, m, :], work[0:M, m, :], start=(m == 0), stop=(m == 2))
                    mm.then_inc(ft_psum, 1)
                    pe.wait_ge(ft_ready, 4 * c + 4)
                    pe.wait_ge(fwT_ready, 1)
                    if c >= 1:
                        pe.wait_ge(br_ready, c)
                    pe.matmul(ps[0:HEADS, 4, :], fawT[:], fs[:], start=True, stop=True).then_inc(br_psum, 1)

            pe.wait_ge(const_in, 16 * N_CONST)
            pe.wait_ge(consts_ready, 1)
            weights()
            layernorm(0)
            pe.wait_ge(aux_ready, 1)
            pe.wait_ge(yt_ready, NC)
            attention(LAYERS[0])
            layernorm(1)
            pe.wait_ge(yt_ready, 2 * NC)
            experts()
            layernorm(2)
            pe.wait_ge(yt_ready, 3 * NC)
            attention(LAYERS[1])
            layernorm(3)
            channel_mix()
            layernorm(4)
            l2_attention()
            layernorm(5)
            mlp(0, 5)
            layernorm(6)
            features()
            pe.wait_ge(aux_ready, 2)
            attention(LAYERS[2])
            layernorm(7)
            mlp(1, 7)

        @block.scalar
        def _(act):
            def layernorm(k):
                act.wait_ge(var_ready, k + 1)
                act.activation(sd[:], stats[:, :, 0], ACT.Sqrt).then_inc(sd_ready, 1)
                for c in range(NC):
                    act.wait_ge(yt_psum, k * NC + c + 1)
                    act.activation(yv[:, c * CH:(c + 1) * CH], bank(c), ACT.Copy).then_inc(yt_ready, 1)

            def attention(L):
                s = A[L.n]
                with act.Fori(0, PAIRS) as i:
                    for n in range(2 * NC):
                        c, qk = n // 2, n % 2
                        act.wait_ge(s["proj_ready"], i * 8 + n + 1)
                        for h in range(2):
                            r = slice(h * DH, (h + 1) * DH)
                            act.activation((M1, S1)[qk][h][0:DH, c * CH:(c + 1) * CH], ps[r, n % 4, :],
                                           ACT.Identity, bias=bqk[r, qk:qk + 1]).then_inc(s["hi_ready"], 1)
                    for n in range(2 * NT):
                        w = L.keys(n % NT)
                        act.wait_ge(s["sc_ready"], i * 2 * NT + n + 1)
                        if n >= 2:
                            act.wait_ge(s["scan_ready"], i * 2 * NT + n - 1)
                        flat = ps[:, 4 * (n % 2):4 * (n % 2) + 4, :].rearrange("p b k -> p (b k)")
                        act.activation(smax[:, n % 2, 0:w // 2], flat[:, w // 2:w], ACT.Copy).then_inc(s["cp_ready"], 1)
                    for g, (c, j, q0) in enumerate(L.tiles):
                        for h in range(2):
                            k = 2 * g + h
                            act.wait_ge(s["st_ready"], i * (2 * L.G) + k + 1)
                            if k >= SLOTS:
                                act.wait_ge(s["acc_ready"], i * (2 * L.G) + k - SLOTS + 1)
                                act.wait_ge(s["pv_done"], i * L.G + g - SLOTS // 2 + 1)
                            act.activation(work[:, k % SLOTS, q0:CH], ps[:, k % 4, q0:CH], ACT.Exp,
                                           scale=L.scale).then_inc(s["p_ready"], 1)

            layernorm(0)
            attention(LAYERS[0])
            layernorm(1)
            act.wait_ge(dl_ready, 1)
            act.activation(small[:, 2, :, :], small[:, 1, :, :], ACT.Exp).then_inc(ex_ready, 1)
            for t in range(NT):
                act.wait_ge(cT_psum, t + 1)
                if t >= 2:
                    act.wait_ge(xp_psum, t - 1)
                act.activation(coefT[:, t % 2, :], ps[0:E_EXP, 3 + t % 2, 0:P], ACT.Copy).then_inc(cT_ready, 1)
            layernorm(2)
            attention(LAYERS[1])
            layernorm(3)
            for c in range(NC):
                act.wait_ge(r_psum, c + 1)
                act.activation(work[:, 8 + c, :], bank(c % 2), ACT.Sigmoid).then_inc(r_ready, 1)
                act.wait_ge(k_psum, c + 1)
                act.activation(work[:, 12 + c, :], bank(2 + c % 2), ACT.Relu).then_inc(kr_ready, 1)
            layernorm(4)
            layernorm(5)
            for m in range(NC * NJ):
                act.wait_ge(F[0]["h_psum"], m + 1)
                c, j = m // NJ, m % NJ
                act.activation(work[:, j * 4 + c, :], bank(m % 4), ACT.Relu, bias=b1[:, 0, j:j + 1]).then_inc(F[0]["h_ready"], 1)
            layernorm(6)
            act.wait_ge(fw_in, 1)
            act.activation(faw[:, 0:NF], faw[:, 0:NF], ACT.Exp).then_inc(fw_exp, 1)
            for c in range(NC):
                for m in range(3):
                    M = P if m < 2 else FH
                    act.wait_ge(ft_psum, 4 * c + m + 1)
                    if c >= 1:
                        act.wait_ge(ft_psum, 4 * c)
                    act.activation(work[0:M, m, :], ps[0:M, m, :], ACT.Gelu, bias=bext[0:M, m:m + 1]).then_inc(ft_ready, 1)
                act.wait_ge(ft_psum, 4 * c + 4)
                act.activation(fs[:], ps[0:NF, 3, :], ACT.Sigmoid, bias=b2ext[:]).then_inc(ft_ready, 1)
                act.wait_ge(br_psum, c + 1)
                if c >= 1:
                    act.wait_ge(br_out, 16 * c)
                act.activation(brow[:], ps[0:HEADS, 4, :], ACT.Copy, scale=1.0 / LAYERS[2].scale).then_inc(br_ready, 1)
            attention(LAYERS[2])
            layernorm(7)
            for m in range(NC * NJ):
                act.wait_ge(F[1]["h_psum"], m + 1)
                c, j = m // NJ, m % NJ
                act.activation(work[:, j * 4 + c, :], bank(m % 4), ACT.Gelu, bias=b1[:, 1, j:j + 1]).then_inc(F[1]["h_ready"], 1)

        @block.gpsimd
        def _(pool):
            def attention(L):
                s = A[L.n]
                with pool.Fori(0, PAIRS) as i:
                    for n in range(2 * NT):
                        w = L.keys(n % NT)
                        pool.wait_ge(s["scan_ready"], i * 2 * NT + n + 1)
                        pool.tensor_tensor(mcol[:, n:n + 1], scan[:, n % 2, w // 2 - 1:w // 2], zcol[:],
                                           ALU.add).then_inc(s["mcol_ready"], 1)
            for L in LAYERS:
                attention(L)

        @block.vector
        def _(dve):
            steps = [0]

            def link(ins):
                steps[0] += 1
                ins.then_inc(dve_step, 1)
                dve.wait_ge(dve_step, steps[0])

            def layernorm(k, bias=None):
                for t in range(NT):
                    ins = dve.bn_stats(stats[:, t, :], x[:, t, :])
                link(ins)
                for t in range(NT):
                    ins = dve.bn_aggr(mv[:, t, :], stats[:, t, :])
                link(ins)
                dve.tensor_scalar(stats[:, :, 0], mv[:, :, 1], EPS, None, ALU.add).then_inc(var_ready, 1)
                dve.wait_ge(sd_ready, k + 1)
                link(dve.reciprocal(rstd[:], sd[:]))
                for t in range(NT):
                    ins = dve.tensor_scalar(work[:, t // TPC, (t % TPC) * P:(t % TPC + 1) * P], x[:, t, :],
                                            mv[:, t, 0:1], rstd[:, t:t + 1], ALU.subtract, ALU.mult)
                    ins.then_inc(yn_ready, 1)
                if bias is not None:
                    dve.wait_ge(yn_ready, (k + 1) * NT)
                    link(dve.tensor_tensor(x[:], x[:], obias[:, bias:bias + 1, :].to_broadcast([P, NT, D]), ALU.add))

            def attention(L):
                s = A[L.n]
                with dve.Fori(0, PAIRS) as i:
                    for n in range(2 * NC):
                        c, qk = n // 2, n % 2
                        for h in range(2):
                            r = slice(h * DH, (h + 1) * DH)
                            dve.wait_ge(s["hi_ready"], i * 16 + 2 * n + h + 1)
                            hi = (M1, S1)[qk][h][0:DH, c * CH:(c + 1) * CH]
                            lo = (M2[h][0:DH], S2[h][DH:P])[qk][:, c * CH:(c + 1) * CH]
                            dve.scalar_tensor_tensor(lo, ps[r, n % 4, :], bqk[r, qk:qk + 1], hi.bitcast(F32),
                                                     ALU.add, ALU.subtract).then_inc(s["lo_ready"], 1)
                    for n in range(2 * NT):
                        w = L.keys(n % NT)
                        dve.wait_ge(s["cp_ready"], i * 2 * NT + n + 1)
                        if n >= 2:
                            dve.wait_ge(s["mcol_ready"], i * 2 * NT + n - 1)
                        flat = ps[:, 4 * (n % 2):4 * (n % 2) + 4, :].rearrange("p b k -> p (b k)")
                        dve.tensor_tensor_scan(scan[:, n % 2, 0:w // 2], flat[:, 0:w // 2], smax[:, n % 2, 0:w // 2],
                                               LOWEST, ALU.max, ALU.max).then_inc(s["scan_ready"], 1)
                    dve.wait_ge(s["mt_psum"], i + 1)
                    dve.tensor_scalar(mT[:], ps[0:2 * NT, 0, 0:P], -1.0, None, ALU.mult).then_inc(s["mt_ready"], 1)
                    for c in range(NC):
                        dve.wait_ge(s["v_psum"], i * NC + c + 1)
                        dst = V[:, c * TPC:(c + 1) * TPC, :]
                        src = bank(4 + c).rearrange("p (t d) -> p t d", d=P)
                        dve.tensor_tensor(dst, src, bv[:].rearrange("p (o d) -> p o d", o=1).to_broadcast([P, TPC, P]),
                                          ALU.add).then_inc(s["v_ready"], 1)

                    def add(g):
                        c, j, q0 = L.tiles[g]
                        for h in range(2):
                            k = 2 * g + h
                            dve.wait_ge(s["p_ready"], i * (2 * L.G) + k + 1)
                            p = work[:, k % SLOTS, q0:CH]
                            o = acc[:, c % 2, h, q0:CH]
                            if j == 0:
                                if c >= 2:
                                    dve.wait_ge(s["den_ready"], i * NC + c - 1)
                                dve.tensor_copy(o, p).then_inc(s["acc_ready"], 1)
                            else:
                                dve.wait_ge(s["acc_ready"], i * (2 * L.G) + k - 1)
                                dve.tensor_tensor(o, o, p, ALU.add).then_inc(s["acc_ready"], 1)

                    def normalise(c):
                        dve.wait_ge(s["den_ready"], i * NC + c + 1)
                        dve.reciprocal(rinv[:], bank(6)).then_inc(s["rinv_ready"], 1)
                        dve.wait_ge(s["rinv_ready"], i * NC + c + 1)
                        dve.wait_ge(s["pv_done"], i * L.G + L.end[c])
                        if c >= 2:
                            dve.wait_ge(s["op_ready"], i * NC + c)
                        dve.tensor_tensor(oT[:, c % 2, :], bank(4 + c % 2), rinv[:], ALU.mult).then_inc(s["ot_ready"], 1)

                    def add_x(c):
                        dve.wait_ge(s["op_ready"], i * NC + c + 2)
                        xs = x[:, c * TPC:(c + 1) * TPC, :]
                        dve.tensor_tensor(xs, xs, bank(7).rearrange("p (t d) -> p t d", d=P), ALU.add)\
                            .then_inc(s["x_added"], 1)

                    for g in range(L.G):
                        add(g)
                        for c in range(NC - 1):
                            if g == L.end[c] + 2:
                                normalise(c)
                            if g == L.end[c] + 5:
                                add_x(c)
                    normalise(NC - 1)
                    add_x(NC - 1)
                dve.wait_ge(s["x_added"], PAIRS * NC)

            def abs_sum(o, w):
                return dve.tensor_reduce(o, w, AX.X, ALU.add, apply_absolute_value=True)

            def weights():
                dve.wait_ge(const_in, 16 * N_CONST)
                for m in range(2):
                    ins = abs_sum(gam[:, m:m + 1], wt[:, m, :])
                ins.then_inc(gam_in, 1)
                for m in range(2):
                    w = wt[:, 2 + m, :]
                    n = NJ if m == 0 else 1
                    k = FF // n
                    wr = w.rearrange("p (n k) -> p n k", n=n)
                    link(abs_sum(few[:, m, 0:n], wr))
                    link(dve.tensor_scalar(few[:, 2 + m, 0:n], few[:, m, 0:n], 1.0 / k, None, ALU.mult))
                    link(dve.tensor_scalar(wtmp[:], w, 0.0, None, ALU.is_lt))
                    link(dve.scalar_tensor_tensor(work[:, 6, :], w, 0.0, wtmp[:], ALU.is_gt, ALU.subtract))
                    for q in range(n):
                        cs = slice(q * k, (q + 1) * k)
                        ins = dve.scalar_tensor_tensor(work[:, 7, cs], work[:, 6, cs], few[:, 2 + m, q:q + 1], w[:, cs],
                                                       ALU.mult, ALU.subtract)
                    link(ins)
                    dve.tensor_tensor(work[:, 4 + m, :], w, work[:, 7, :], ALU.add).then_inc(wm_ready, 1)
                    dve.wait_ge(wm_ready, m + 1)
                dve.wait_ge(gam_psum, 1)
                link(dve.tensor_scalar(gam[:, 2:4], ps[:, 0, 0:2], 1.0 / (FF * D), EPS, ALU.mult, ALU.add))
                link(dve.tensor_scalar(gam[:, 4:6], gam[:, 2:4], 0.5, None, ALU.mult))
                link(dve.tensor_scalar(gam[:, 6:8], gam[:, 2:4], -0.5, None, ALU.mult))
                for m in range(2):
                    link(dve.tensor_scalar(wtmp[:], wt[:, m, :], gam[:, 6 + m:7 + m], None, ALU.is_lt))
                    link(dve.scalar_tensor_tensor(wm[:, m, :], wt[:, m, :], gam[:, 4 + m:5 + m], wtmp[:],
                                                  ALU.is_gt, ALU.subtract))
                for m in range(2):
                    dve.wait_ge(wT_psum, m + 1)
                    link(dve.tensor_copy(wm[:, 2 + m, :], bank(1 + m)))

            def experts():
                def bc(v):
                    return v.rearrange("p (t o) -> p t o", o=1).to_broadcast([P, NT, E_EXP])
                sm = [small[:, n, :, :] for n in range(8)]
                fw = [few[:, n, :] for n in range(4)]
                dve.wait_ge(lg_ready, 1)
                lg = ps[:, 0, 0:P].rearrange("p (t e) -> p t e", e=E_EXP)
                link(dve.tensor_copy(sm[0], lg))
                link(dve.tensor_reduce(fw[0], sm[0], AX.X, ALU.max))
                dve.tensor_tensor(sm[1], sm[0], bc(fw[0]), ALU.subtract).then_inc(dl_ready, 1)
                dve.wait_ge(ex_ready, 1)
                link(dve.tensor_reduce(fw[1], sm[2], AX.X, ALU.add))
                link(dve.reciprocal(fw[2], fw[1]))
                link(dve.tensor_tensor(sm[3], sm[2], bc(fw[2]), ALU.mult))
                link(dve.tensor_reduce(fw[3], sm[3], AX.X, ALU.max))
                link(dve.tensor_tensor(sm[0], sm[3], bc(fw[3]), ALU.is_ge))
                link(dve.tensor_tensor(sm[1], sm[0], first[:].rearrange("p (o e) -> p o e", o=1)
                                       .to_broadcast([P, NT, E_EXP]), ALU.mult))
                link(dve.tensor_reduce(fw[0], sm[1], AX.X, ALU.max))
                dve.tensor_tensor(sm[4], sm[1], bc(fw[0]), ALU.is_equal).then_inc(mask_ready, 1)
                dve.wait_ge(loc_psum, 1)
                tot = ps[:, 2, 0:P].rearrange("p (t e) -> p t e", e=E_EXP)
                link(dve.tensor_copy(sm[6], tot))
                src, dst = 6, 7
                for k in (1, 2, 4, 8):
                    link(dve.tensor_tensor(sm[dst][:, k:NT, :], sm[src][:, k:NT, :], sm[src][:, 0:NT - k, :], ALU.add))
                    link(dve.tensor_copy(sm[dst][:, 0:k, :], sm[src][:, 0:k, :]))
                    src, dst = dst, src
                link(dve.tensor_tensor(sm[0], sm[src], tot, ALU.subtract))
                link(dve.tensor_tensor(sm[1], sm[0], ps[:, 1, 0:P].rearrange("p (t e) -> p t e", e=E_EXP), ALU.add))
                link(dve.tensor_scalar(sm[2], sm[1], float(CAP), None, ALU.is_lt))
                link(dve.tensor_tensor(sm[0], sm[2], sm[4], ALU.mult))
                dve.tensor_tensor(sm[5], sm[0], sm[3], ALU.mult).then_inc(cf_ready, 1)
                dve.wait_ge(cf_ready, 1)
                for t in range(NT):
                    dve.wait_ge(xp_psum, t + 1)
                    b0 = 6 if t % 2 == 0 else 0
                    link(dve.tensor_tensor(x[:, t, :], x[:, t, :], ps[:, 5 if t % 2 == 0 else 2, 0:D], ALU.add))
                    for e in range(E_EXP):
                        dve.scalar_tensor_tensor(x[:, t, :], ps[:, b0 + e // 4, (e % 4) * D:(e % 4 + 1) * D],
                                                 sm[5][:, t, e:e + 1], x[:, t, :], ALU.mult, ALU.add).then_inc(x_exp, 1)
                        dve.wait_ge(x_exp, t * E_EXP + e + 1)

            def channel_mix():
                dve.wait_ge(yt_ready, 4 * NC)
                for c in range(NC):
                    cur = yT[:, 1 + c * CH:1 + (c + 1) * CH]
                    prev = yT[:, c * CH:(c + 1) * CH]
                    for m in range(2):
                        link(dve.tensor_scalar(rinv[:], cur, mu[:, m:m + 1], None, ALU.mult))
                        t1 = rinv[:]
                        dve.scalar_tensor_tensor(work[:, 4 * m + c, :], prev, mu[:, 2 + m:3 + m], t1,
                                                 ALU.mult, ALU.add).then_inc(mix_ready, 1)
                        dve.wait_ge(mix_ready, 2 * c + m + 1)
                for c in range(NC):
                    dve.wait_ge(kr_ready, c + 1)
                    dve.tensor_tensor(work[:, 4 + c, :], work[:, 12 + c, :], work[:, 12 + c, :], ALU.mult).then_inc(k_ready, 1)
                for c in range(NC):
                    dve.wait_ge(mo_psum, c + 1)
                    dve.wait_ge(r_ready, c + 1)
                    link(dve.tensor_tensor(work[:, 12 + c, :], bank(4 + c), work[:, 8 + c, :], ALU.mult))
                    xs = x[:, c * TPC:(c + 1) * TPC, :]
                    link(dve.tensor_tensor(xs, xs, work[:, 12 + c, :].rearrange("p (t d) -> p t d", d=D), ALU.add))

            def l2_attention():
                dve.wait_ge(l2_psum, 1)
                dve.scalar_tensor_tensor(l2[:, 0, :], ps[:, 4, 0:D], float(8) ** -0.5, wl2[:, 4, :],
                                         ALU.mult, ALU.mult).then_inc(l2_ready, 1)
                for m in range(2):
                    dve.wait_ge(l2_psum, 2 + m)
                    dve.tensor_copy(l2[:, 1 + m, :], ps[:, 5 + m, 0:D]).then_inc(l2_ready, 1)
                add_out(lo_psum, 0)

            def add_out(ready, b0, done=None):
                for c in range(NC):
                    dve.wait_ge(ready, c + 1)
                    xs = x[:, c * TPC:(c + 1) * TPC, :]
                    ins = dve.tensor_tensor(xs, xs, bank(b0 + c).rearrange("p (t d) -> p t d", d=D), ALU.add)
                    if done is not None:
                        ins.then_inc(done, 1)
                    else:
                        link(ins)

            def features():
                link(dve.tensor_reduce(faw[:, 5:6], faw[:, 0:NF], AX.X, ALU.max))
                dve.tensor_scalar(faw[:, 0:NF], faw[:, 0:NF], faw[:, 5:6], None, ALU.subtract).then_inc(fw_in, 1)
                dve.wait_ge(fw_exp, 1)
                link(dve.tensor_reduce(faw[:, 6:7], faw[:, 0:NF], AX.X, ALU.add))
                link(dve.reciprocal(faw[:, 7:8], faw[:, 6:7]))
                dve.tensor_scalar(faw[:, 0:NF], faw[:, 0:NF], faw[:, 7:8], None, ALU.mult).then_inc(fw_ready, 1)
                dve.wait_ge(fwT_psum, 1)
                dve.tensor_copy(fawT[:], ps[0:NF, 7, 0:HEADS]).then_inc(fwT_ready, 1)

            def auxiliary_rows():
                dve.wait_ge(aux_in, 16)
                aux = V[:].rearrange("p t d -> p (t d)")
                for h in range(2):
                    dve.tensor_copy(S1[h][DH:P, :], aux[DH:P, :])
                    ins = dve.tensor_copy(M1[h][DH:P, :], aux[0:DH, :])
                ins.then_inc(aux_ready, 1)
                dve.wait_ge(aux_ready, 2)

            for h in range(2):
                for m in (M1[h], S1[h]):
                    ins = dve.memset(m[DH:P, :].bitcast(F32), 0.0)
            link(ins)
            for h in range(2):
                ins = dve.memset(S1[h][ROW_M:ROW_M + 1, :].bitcast(F32), 1.0)
            ins.then_inc(aux_ready, 1)
            dve.memset(yT[:, 0:1], 0.0)
            dve.memset(zcol[:], 0.0)
            dve.memset(zrow[:], 0.0)
            dve.memset(ones[:], 1.0).then_inc(consts_ready, 1)
            weights()
            for dst, src in ((identb, ident), (maskqsb, maskqs), (masksqb, masksq)):
                dve.tensor_copy(dst[:], src[:])
            dve.tensor_scalar(mu[:, 2:4], mu[:, 0:2], -1.0, 1.0, ALU.mult, ALU.add)
            for m in range(3):
                dve.tensor_scalar(w2b[:, m, :], w2m[:, m, :], w2ext[:, m:m + 1], None, ALU.mult)
            dve.wait_ge(x_in, 16)
            layernorm(0, bias=0)
            attention(LAYERS[0])
            layernorm(1)
            experts()
            link(dve.memset(bqk[:], 0.0))
            link(dve.memset(bv[:], 0.0))
            layernorm(2, bias=1)
            attention(LAYERS[1])
            layernorm(3)
            channel_mix()
            layernorm(4, bias=2)
            l2_attention()
            layernorm(5, bias=3)
            add_out(F[0]["f_psum"], 4)
            layernorm(6, bias=4)
            features()
            auxiliary_rows()
            attention(LAYERS[2])
            layernorm(7, bias=5)
            add_out(F[1]["f_psum"], 4, done=F[1]["f_used"])


def constants():
    f = np.float32
    i = np.arange(P)
    c = {"c_ident": np.eye(P, dtype=f)}
    c["c_maskqs"] = np.where(i[None, :] > i[:, None], f(-BIG), f(0))
    c["c_masksq"] = np.ascontiguousarray(c["c_maskqs"].T)
    c["c_before"] = (i[:, None] < i[None, :]).astype(f)
    c["c_first"] = np.tile(E_EXP - np.arange(E_EXP, dtype=f), (P, 1))
    c["c_block"] = (i[:, None] // 8 == i[None, :] // 8).astype(f)
    h = np.arange(3 * P).reshape(3, P).T
    c["c_w2m"] = (h[:, :, None] // FH == np.arange(NF)).astype(f)
    allowed = np.zeros((T, T), bool)
    for r, chans in enumerate(REGIONS):
        ch = [k + 6 for k in chans]
        allowed[r, ch] = True
        allowed[ch, r] = True
    allowed[:NREG, :NREG] = True
    allowed[NREG:, NREG:] = True
    keys, queries = np.zeros((DH, T), f), np.zeros((DH, T), f)
    keys[ROW_M - DH] = keys[ROW_B - DH] = 1
    for r in range(NREG):
        keys[ROW_R - DH + r, r] = 1
        queries[ROW_R - DH + r] = np.where(allowed[:, r], 0, -BIG)
        keys[ROW_C - DH + r, NREG:] = np.where(allowed[r, NREG:], 0, 1)
        queries[ROW_C - DH + r, r] = -BIG
    c["c_aux"] = np.concatenate([queries, keys])
    return c


def laid_out(i):
    flat = lambda w: np.ascontiguousarray(w.reshape(HEADS * DH, D).T)
    d = {k: i[k] for k in (
        "L0_attn_x", "L0_attn_b_O", "L1_attn_b_u", "L2_attn_out_b", "L2_ffn_b2", "L3_attn_out_b", "L3_ffn_b2",
        "L0_ffn_wg", "L0_ffn_b", "L1_ffn_mu_r", "L1_ffn_mu_k", "L1_attn_w_q", "L1_attn_w_k", "L1_attn_w_v",
        "L1_attn_w_u", "L3_attn_qkv_w", "L3_attn_out_w", "L3_attn_ext_b2", "L3_attn_faw")}
    d["L0_wq"], d["L0_wk"], d["L0_wv"] = flat(i["L0_attn_W_Q"]), flat(i["L0_attn_W_K"]), flat(i["L0_attn_W_V"])
    d["L0_wo"] = i["L0_attn_W_O"].transpose(0, 2, 1).reshape(HEADS * DH, D)
    d["L0_bq"], d["L0_bk"] = i["L0_attn_b_Q"].reshape(-1, 1), i["L0_attn_b_K"].reshape(-1, 1)
    d["L0_bv"] = i["L0_attn_b_V"].reshape(1, -1)
    d["L0_wexp"] = i["L0_ffn_W"].transpose(2, 0, 1)
    d["L1_wmix"] = np.stack([i["L1_ffn_W_r"].T, i["L1_ffn_W_k"].T, i["L1_ffn_W_v"].T], 1)
    q, v = i["L2_attn_q_weight"].reshape(D, D), i["L2_attn_v_weight"].reshape(D, D)
    d["L2_w"] = np.stack([q, v, q.T, i["L2_attn_out_w"].T], 1)
    tiles = lambda w: w.reshape(NJ, P, D).transpose(1, 0, 2).reshape(P, FF)
    d["mlp_w"] = np.stack([i["L2_ffn_W1"].T, tiles(i["L2_ffn_W2"].T), tiles(i["L3_ffn_w1"]), i["L3_ffn_w2"]], 1)
    d["mlp_b1"] = np.stack([i["L2_ffn_b1"].reshape(NJ, P).T, i["L3_ffn_b1"].reshape(NJ, P).T], 1)
    d["L3_wext"] = i["L3_attn_ext_w1"].transpose(1, 0, 2).reshape(D, NF * FH)

    def hidden(w):
        o = np.zeros((3 * P,), np.float32)
        o[:NF * FH] = w.reshape(-1)
        return o.reshape(3, P).T
    d["L3_bext"], d["L3_w2ext"] = hidden(i["L3_attn_ext_b1"]), hidden(i["L3_attn_ext_w2"])
    return d


def kernel(**inputs):
    import concourse.bacc as bacc
    from concourse.bass_utils import run_bass_kernel_spmd

    nc = bacc.Bacc("TRN2", target_bir_lowering=False, num_devices=1)
    inputs = {k: np.asarray(v) for k, v in inputs.items()}
    arrays, aps = {}, {}
    for name, v in {**laid_out(inputs), **constants()}.items():
        v = np.ascontiguousarray(v)
        arrays["in_" + name] = v
        aps[name] = nc.dram_tensor("in_" + name, v.shape, mybir.dt.from_np(v.dtype), kind="ExternalInput").ap()
    out = nc.dram_tensor("out_x", [1, T, D], F32, kind="ExternalOutput").ap()
    program(nc, aps, out)
    r = run_bass_kernel_spmd(nc, [arrays], core_ids=[0])
    return r.results[0]["out_x"]
```

```python
from contextlib import ExitStack

import numpy as np

import concourse.bass as bass
from concourse import mybir

F32 = mybir.dt.float32
F32R = mybir.dt.float32r
BF16 = mybir.dt.bfloat16
ALU = mybir.AluOpType
ACT = mybir.ActivationFunctionType
AX = mybir.AxisListType

P = 128
T = 2048
D = 128
NT = T // P
CH = 512
NC = T // CH
TPC = CH // P
HEADS, DH = 16, 64
PAIRS = HEADS // 2
E_EXP = 8
CAP = T // E_EXP
FF = 512
NJ = FF // P
EPS = 1e-5
BIG = 2.0 ** 100
LOWEST = -3.0e38
NREG = 7
REGIONS = [[1, 4, 10], [40, 47, 52], [2, 3, 5, 7, 8, 13], [44, 46, 49, 50, 51, 53],
           [6, 11, 14, 17, 18, 20, 25, 31, 32, 34, 39, 42, 45], [12, 24, 26, 38],
           [9, 15, 16, 19, 21, 22, 23, 27, 28, 29, 30, 33, 35, 36, 37, 41, 43, 48]]
NF, FH = 5, 64
ROW_M, ROW_B, ROW_R, ROW_C = 64, 65, 66, 73

SLOTS = 16
MISC, OUT = 2, 3


def at_least(engine, sem, value):
    if not (isinstance(value, int) and value <= 0):
        engine.wait_ge(sem, value)


def each_stage(fori, stage):
    stage(-1, 1, main=False, prep=True, tail=False)
    stage(0, 0, main=True, prep=True, tail=False)
    stage(0, 1, main=True, prep=True, tail=True)
    with fori(1, PAIRS - 1) as i:
        stage(i, 0, main=True, prep=True, tail=True)
        stage(i, 1, main=True, prep=True, tail=True)
    stage(PAIRS - 1, 0, main=True, prep=True, tail=True)
    stage(PAIRS - 1, 1, main=True, prep=False, tail=True)


class Layer:

    def __init__(self, n, causal, scale, biased, featured):
        self.n, self.causal, self.scale = n, causal, scale
        self.biased, self.featured = biased, featured
        self.steps = []
        for c in range(NC):
            for j in range(0, TPC * (c + 1) if causal else NT, 2):
                two = []
                for jj in (j, j + 1):
                    r = jj - TPC * c
                    if not causal or r < 0:
                        two.append((jj, 0, None, None))
                    elif jj == 1:
                        two.append((jj, 0, 0, P))
                    else:
                        two.append((jj, r * P, None, r * P))
                self.steps.append((c, two))
        self.K = len(self.steps)
        self.end = [max(k for k, st in enumerate(self.steps) if st[0] == c) + 1 for c in range(NC)]
        self.first = [0] + self.end[:-1]
        self.maxima = []
        for t in range(NT):
            w = (t + 1) * P if causal else T
            for k0 in range(0, w, T // 2):
                self.maxima.append((t, k0, min(T // 2, w - k0), k0 + T // 2 >= w))
        self.NM = len(self.maxima)
        m0 = 6 if causal else 9
        self.at = [m0 + m * (self.K - m0) // self.NM for m in range(self.NM)]
        self.qk_at = (0, 2, 3, 5) if causal else (0, 2, 5, 8)
        self.prep_jobs = [(k, "qk", c) for c, k in enumerate(self.qk_at)] + [(12 if causal else 22, "mt", 0)]
        self.v_jobs = [(k, "v", c) for c, k in enumerate((7, 9, 13, 17) if causal else (10, 15, 17, 24))]
        gap = 2 if causal else 3
        self.main_jobs = [(1 if causal else 3, "mt", 1)]
        for c in range(NC - 1):
            self.main_jobs += [(self.end[c] + gap, "den", c), (self.end[c] + gap + 2, "op", c)]
        self.tail_jobs = [(1, "den", NC - 1), (3 if causal else 6, "op", NC - 1)]
        self.qk_loads = 2 if biased else 1
        self.rows = 2 if featured else 1

    def jobs(self, i, p, main, prep, tail):
        n = 2 * i + p
        found = []
        if tail:
            found += [(k, kind, n - 1, c, 1 - p) for k, kind, c in self.tail_jobs]
        if prep:
            found += [(k, kind, n + 1, c, 1 - p) for k, kind, c in self.prep_jobs]
            if p == 1:
                found += [(k, kind, i + 1, c, 0) for k, kind, c in self.v_jobs]
        if main:
            found += [(k, kind, n, c, p) for k, kind, c in self.main_jobs]
        return sorted(found, key=lambda f: f[0])

    def at_step(self, k):
        return [m for m in range(self.NM) if self.at[m] == k]

    def finals(self, m):
        return sum(f for _, _, _, f in self.maxima[:max(m, 0)])


LAYERS = [Layer(0, False, 0.125, True, False), Layer(1, True, 1.0 / 64, False, False),
          Layer(2, False, 0.125, False, True)]


def program(nc, a, out):
    with ExitStack() as ctx:
        def sb(name, shape, dt=F32):
            return ctx.enter_context(nc.sbuf_tensor(name, shape, dt))

        def sem(name):
            return ctx.enter_context(nc.semaphore(name))

        x = sb("x", [P, NT, D])
        yT = sb("yT", [P, T + 2])
        S1 = [sb(f"S1_{h}", [P, T], F32R) for h in range(2)]
        M1 = [sb(f"M1_{h}", [P, T], F32R) for h in range(2)]
        S2 = [sb(f"S2_{h}", [P, T], F32R) for h in range(2)]
        M2 = [sb(f"M2_{h}", [P, T], F32R) for h in range(2)]
        V = [sb(f"V_{p}", [P, NT, DH]) for p in range(2)]
        Vnext = sb("Vnext", [P, NT, DH])
        work = sb("work", [P, SLOTS, CH])
        acc = sb("acc", [P, 2, CH])
        smax = sb("smax", [P, 2, CH])
        scan = sb("scan", [P, 2, CH])
        mcol = sb("mcol", [P, NT])
        mT = sb("mT", [NT // 2, 2, P], F32R)
        oT = sb("oT", [P, 2, CH])
        rinv = sb("rinv", [P, 2, TPC])
        mixed = sb("mixed", [P, CH])
        wqk = [sb(f"wqk_{p}", [P, P]) for p in range(2)]
        wv = sb("wv", [P, P])
        wo = [sb(f"wo_{p}", [P, D]) for p in range(2)]
        bqk = sb("bqk", [P, 2])
        bv = sb("bv", [P, P])
        zrow = sb("zrow", [1, 1, CH])
        zcol = sb("zcol", [P, 1])
        ident = sb("ident", [P, P])
        identb = sb("identb", [P, P], BF16)
        maskqs = sb("maskqs", [P, P])
        masksq = sb("masksq", [P, P])
        maskqsb = sb("maskqsb", [P, P], BF16)
        masksqb = sb("masksqb", [P, P], BF16)
        allb = sb("allb", [P, P], BF16)
        before = sb("before", [P, P])
        ones = sb("ones", [P, P])
        obias = sb("obias", [P, 6, D])
        stats = sb("stats", [P, NT, 6])
        mv = sb("mv", [P, NT, 2])
        sd = sb("sd", [P, NT])
        rstd = sb("rstd", [P, NT])
        wg = sb("wg", [P, E_EXP])
        wexp = sb("wexp", [P, E_EXP, D])
        bexp = sb("bexp", [E_EXP, D])
        first = sb("first", [P, E_EXP])
        small = sb("small", [P, 8, NT, E_EXP])
        few = sb("few", [P, 4, NT])
        coefT = sb("coefT", [E_EXP, 2, P])
        wmix = sb("wmix", [P, 3, D])
        mu = sb("mu", [P, 4])
        wl2 = sb("wl2", [P, 5, D])
        l2 = sb("l2", [P, 3, D])
        wt = sb("wt", [P, 4, FF])
        wm = sb("wm", [P, 4, FF])
        wtmp = sb("wtmp", [P, FF])
        b1 = sb("b1", [P, 2, NJ])
        gam = sb("gam", [P, 8])
        wext = sb("wext", [P, NF * FH])
        bext = sb("bext", [P, 3])
        w2ext = sb("w2ext", [P, 3])
        w2m = sb("w2m", [P, 3, NF])
        w2b = sb("w2b", [P, 3, NF])
        b2ext = sb("b2ext", [NF, 1])
        faw = sb("faw", [HEADS, 8])
        fawT = sb("fawT", [NF, HEADS])
        fs = sb("fs", [NF, CH])
        brow = sb("brow", [HEADS, CH])
        brow_dram = nc.dram_tensor("bias_rows", [HEADS, T], F32, kind="Internal").ap()

        ps = ctx.enter_context(nc.psum_tensor("ps", [P, 8, CH], F32))

        def bank(b):
            return ps[:, b, :]

        yv = yT[:, 1:T + 1]

        const_in = sem("const_in")
        x_in = sem("x_in")
        dve_step = sem("dve_step")
        consts_ready = sem("consts_ready")
        var_ready = sem("var_ready")
        sd_ready = sem("sd_ready")
        yn_ready = sem("yn_ready")
        yt_psum = sem("yt_psum")
        yt_ready = sem("yt_ready")
        out_done = sem("out_done")

        A = [{k: sem(f"{k}_{L.n}") for k in (
            "wqk_in", "wv_in", "wo_in",
            "zero_done",
            "proj_ready",
            "hi_ready",
            "lo_ready",
            "dup_done",
            "sc_ready",
            "cp_ready",
            "scan_ready",
            "mcol_ready",
            "mt_psum",
            "mt_ready",
            "mrow_done",
            "v_psum",
            "v_ready",
            "vcopy_done",
            "st_ready",
            "p_ready",
            "acc_ready",
            "pv_done",
            "o_ready",
            "den_ready",
            "rinv_ready",
            "op_ready",
            "x_added",
        )} for L in LAYERS]
        aux_ready = sem("aux_ready")
        aux_in = sem("aux_in")
        row_ready = sem("row_ready")
        fw_in, fw_exp = sem("fw_in"), sem("fw_exp")
        lg_ready, dl_ready, ex_ready, mask_ready, loc_psum, cf_ready = (
            sem(s) for s in ("lg_ready", "dl_ready", "ex_ready", "mask_ready", "loc_psum", "cf_ready"))
        cT_psum, cT_ready, xp_psum, xp_used, x_exp = (
            sem(s) for s in ("cT_psum", "cT_ready", "xp_psum", "xp_used", "x_exp"))
        mix_ready, r_psum, r_ready, k_psum, kr_ready, k_ready, mo_psum, mo_used = (
            sem(s) for s in ("mix_ready", "r_psum", "r_ready", "k_psum", "kr_ready", "k_ready",
                             "mo_psum", "mo_used"))
        l2_psum, l2_ready, lo_psum, lo_used = (
            sem(s) for s in ("l2_psum", "l2_ready", "lo_psum", "lo_used"))
        gam_in, gam_psum, wm_ready, wT_psum, wT_ready = (
            sem(s) for s in ("gam_in", "gam_psum", "wm_ready", "wT_psum", "wT_ready"))
        F = [{k: sem(f"{k}_{n}") for k in ("h_psum", "h_ready", "f_psum", "f_used")} for n in range(2)]
        ft_psum, ft_ready, fw_ready, fwT_psum, fwT_ready, br_psum, br_ready, br_out = (
            sem(s) for s in ("ft_psum", "ft_ready", "fw_ready", "fwT_psum", "fwT_ready", "br_psum",
                             "br_ready", "br_out"))

        block = ctx.enter_context(nc.Block())

        wouts = ["L0_wo", "L1_attn_w_u", "L3_attn_out_w"]

        def rows(ap, n=P):
            return ap.rearrange("(o d) -> o d", o=1).to_broadcast([n, ap.shape[0]])

        def column(ap):
            return ap.rearrange("(p o) -> p o", o=1)

        const_loads = [
            (ident[:], a["c_ident"]), (maskqs[:], a["c_maskqs"]), (masksq[:], a["c_masksq"]),
            (wt[:], a["mlp_w"]), (b1[:], a["mlp_b1"]),
            (before[:], a["c_before"]), (first[:], a["c_first"]), (wl2[:, 4, :], a["c_block"]),
            (wg[:], a["L0_ffn_wg"]), (wexp[:], a["L0_wexp"]), (bexp[:], a["L0_ffn_b"]),
            (wmix[:], a["L1_wmix"]), (mu[:, 0:1], column(a["L1_ffn_mu_r"])), (mu[:, 1:2], column(a["L1_ffn_mu_k"])),
            (wl2[:, 0:4, :], a["L2_w"]),
            (wext[:], a["L3_wext"]), (bext[:], a["L3_bext"]), (w2ext[:], a["L3_w2ext"]), (w2m[:], a["c_w2m"]),
            (b2ext[:], column(a["L3_attn_ext_b2"])), (faw[:, 0:NF], a["L3_attn_faw"]),
        ] + [(obias[:, n, :], rows(a[k])) for n, k in enumerate(
            ("L0_attn_b_O", "L1_attn_b_u", "L2_attn_out_b", "L2_ffn_b2", "L3_attn_out_b", "L3_ffn_b2"))]
        N_CONST = len(const_loads)

        @block.sync
        def _(sp):
            sp.dma_start(x[:], a["L0_attn_x"].rearrange("b (t p) d -> p (b t) d", p=P)).then_inc(x_in, 16)
            for dst, src in const_loads:
                sp.dma_start(dst, src).then_inc(const_in, 16)

            sp.wait_ge(consts_ready, 1)
            def attention(L):
                s = A[L.n]

                def load_qk(i, p):
                    h = 2 * i + p
                    sp.dma_start(wqk[p][:], a[f"wqk_{L.n}"][:, bass.ds(h * P, P)]).then_inc(s["wqk_in"], 16)
                    if L.biased:
                        sp.dma_start(bqk[:, p:p + 1], a["L0_bqk"][bass.ds(h * P, P), :]).then_inc(s["wqk_in"], 16)

                def load_v(u):
                    sp.dma_start(wv[:], a[f"wv_{L.n}"][:, bass.ds(u * P, P)]).then_inc(s["wv_in"], 16)
                    if L.biased:
                        sp.dma_start(bv[:], a["L0_bv"][:, bass.ds(u * P, P)].to_broadcast([P, P])).then_inc(s["wv_in"], 16)

                def stage(i, p, main, prep, tail):
                    n = 2 * i + p
                    m, q = n + 1, 1 - p
                    if main:
                        if p == 0:
                            sp.wait_ge(s["v_ready"], 8 * i + 8)
                            at_least(sp, s["pv_done"], L.K * n)
                            sp.dma_start(V[1][:], Vnext[:]).then_inc(s["vcopy_done"], 16)
                        sp.wait_ge(s["mt_ready"], 2 * n + 2)
                        sp.dma_start(M1[p][ROW_M:ROW_M + 1, T // 2:].bitcast(F32).rearrange("o (t p) -> o t p", p=P),
                                     mT[:, 1, :].bitcast(F32)).then_inc(s["mrow_done"], 16)
                    if not prep:
                        return
                    at_least(sp, s["st_ready"], 2 * L.K * n)
                    sp.dma_start(M1[q][ROW_M:ROW_M + 1, :].bitcast(F32).rearrange("o (c q) -> o c q", c=NC),
                                 zrow[:].to_broadcast([1, NC, CH])).then_inc(s["zero_done"], 16)
                    if L.featured:
                        sp.dma_start(M1[q][ROW_B:ROW_B + 1, :].bitcast(F32),
                                     brow_dram[bass.ds(m, 1), :]).then_inc(s["zero_done"], 16)
                    at_least(sp, s["op_ready"], NC * n)
                    for half in range(2):
                        sp.dma_start(wo[q][half * DH:(half + 1) * DH, :],
                                     a[wouts[L.n]][bass.ds(m * DH, DH), :]).then_inc(s["wo_in"], 16)
                    sp.wait_ge(s["hi_ready"], 8 * m + 8)
                    sp.dma_start(M2[q][DH:P, :].bitcast(F32), M1[q][0:DH, :].bitcast(F32)).then_inc(s["dup_done"], 16)
                    sp.dma_start(S2[q][0:DH, :].bitcast(F32), S1[q][0:DH, :].bitcast(F32)).then_inc(s["dup_done"], 16)
                    if not (isinstance(i, int) and i == PAIRS - 1):
                        if main:
                            sp.wait_ge(s["lo_ready"], 8 * n + 8)
                        load_qk(i + 1, p) if main else load_qk(0, 1)
                        if p == 0:
                            sp.wait_ge(s["v_ready"], 8 * i + 8)
                            load_v(i + 1)
                    sp.wait_ge(s["mt_ready"], 2 * m + 1)
                    sp.dma_start(M1[q][ROW_M:ROW_M + 1, 0:T // 2].bitcast(F32).rearrange("o (t p) -> o t p", p=P),
                                 mT[:, 0, :].bitcast(F32)).then_inc(s["mrow_done"], 16)

                load_qk(0, 0)
                load_v(0)
                each_stage(sp.Fori, stage)

            attention(LAYERS[0])
            sp.wait_ge(A[0]["op_ready"], NC * HEADS)
            attention(LAYERS[1])
            sp.wait_ge(A[1]["op_ready"], NC * HEADS)
            sp.wait_ge(F[0]["f_psum"], NC)
            sp.dma_start(work[:, 8:8 + NC, :].rearrange("p c q -> p (c q)"), a["c_aux"]).then_inc(aux_in, 16)
            for c in range(NC):
                sp.wait_ge(br_ready, c + 1)
                sp.dma_start(brow_dram[:, c * CH:(c + 1) * CH], brow[:]).then_inc(br_out, 16)
            sp.wait_ge(br_out, 16 * NC)
            sp.wait_ge(aux_ready, 2)
            attention(LAYERS[2])
            sp.wait_ge(F[1]["f_used"], NC)
            sp.dma_start(out.rearrange("b (t p) d -> p (b t) d", p=P), x[:]).then_inc(out_done, 16)
            sp.wait_ge(out_done, 16)

        @block.tensor
        def _(pe):
            def layernorm(k):
                for t in range(NT):
                    pe.wait_ge(yn_ready, k * NT + t + 1)
                    mm = pe.transpose(ps[:, t // TPC, (t % TPC) * P:(t % TPC + 1) * P],
                                      work[:, t // TPC, (t % TPC) * P:(t % TPC + 1) * P], ident[:])
                    if t % TPC == TPC - 1:
                        mm.then_inc(yt_psum, 1)

            def attention(L):
                s = A[L.n]
                K, NM = L.K, L.NM

                def released(kind, h, c):
                    if kind == "qk":
                        pe.wait_ge(s["lo_ready"], 8 * h + 2 * c + 2)
                    elif kind == "v":
                        pe.wait_ge(s["v_ready"], 8 * h + 2 * c + 2)
                    elif kind == "mt":
                        pe.wait_ge(s["mt_ready"], 2 * h + c + 1)
                    elif kind == "den":
                        pe.wait_ge(s["rinv_ready"], NC * h + c + 1)
                    else:
                        pe.wait_ge(s["x_added"], NT * h + TPC * c + TPC)

                def job(kind, h, c, p):
                    if kind == "qk":
                        if c == 0:
                            pe.wait_ge(s["wqk_in"], 16 * L.qk_loads * h + 16 * L.qk_loads)
                        pe.matmul(bank(MISC), wqk[p][:], yv[:, c * CH:(c + 1) * CH],
                                  start=True, stop=True).then_inc(s["proj_ready"], 1)
                    elif kind == "v":
                        if c == 0:
                            pe.wait_ge(s["wv_in"], 16 * L.qk_loads * h + 16 * L.qk_loads)
                        for t in range(TPC):
                            mm = pe.matmul(ps[:, MISC, t * P:(t + 1) * P],
                                           yv[:, (c * TPC + t) * P:(c * TPC + t + 1) * P], wv[:],
                                           start=True, stop=True)
                        mm.then_inc(s["v_psum"], 1)
                    elif kind == "mt":
                        pe.wait_ge(s["mcol_ready"], NT * h + NT // 2 * (c + 1))
                        pe.transpose(ps[0:NT // 2, MISC, 0:P], mcol[:, NT // 2 * c:NT // 2 * (c + 1)],
                                     ident[:]).then_inc(s["mt_psum"], 1)
                    elif kind == "den":
                        pe.wait_ge(s["acc_ready"], 2 * K * h + 2 * L.end[c])
                        for t in range(TPC):
                            mm = pe.matmul(ps[:, MISC, t * P:(t + 1) * P], acc[:, c % 2, t * P:(t + 1) * P], ones[:],
                                           start=True, stop=True)
                        mm.then_inc(s["den_ready"], 1)
                    else:
                        if c == 0:
                            pe.wait_ge(s["wo_in"], 32 * h + 32)
                        pe.wait_ge(s["o_ready"], NC * h + c + 1)
                        for t in range(TPC):
                            mm = pe.matmul(ps[:, MISC, t * P:(t + 1) * P], oT[:, c % 2, t * P:(t + 1) * P], wo[p][:],
                                           start=True, stop=True)
                        mm.then_inc(s["op_ready"], 1)

                def scores(n, p, k, h2):
                    c, two = L.steps[k]
                    j, q0, whole, diag = two[h2]
                    at_least(pe, s["p_ready"], 2 * K * n + 2 * k + h2 - 1)
                    o = ps[:, h2, q0:CH]
                    pe.matmul(o, S1[p][:, j * P:(j + 1) * P], M1[p][:, c * CH + q0:(c + 1) * CH],
                              start=True, stop=False)
                    mm = pe.matmul(o, S2[p][:, j * P:(j + 1) * P], M2[p][:, c * CH + q0:(c + 1) * CH],
                                   start=False, stop=diag is None)
                    if whole is not None:
                        pe.matmul(ps[:, h2, whole:whole + P], identb[:], allb[:], start=False, stop=False)
                    if diag is not None:
                        mm = pe.matmul(ps[:, h2, diag:diag + P], identb[:], masksqb[:], start=False, stop=True)
                    mm.then_inc(s["st_ready"], 1)

                def maximum(h, p, m):
                    t, k0, w, _ = L.maxima[m]
                    if m == 0:
                        pe.wait_ge(s["zero_done"], 16 * L.rows * h + 16 * L.rows)
                        pe.wait_ge(s["hi_ready"], 8 * h + 8)
                    at_least(pe, s["scan_ready"], NM * h + m - 1)
                    b = 4 + 2 * (m % 2)
                    for j in range(0, w, CH):
                        cols = min(CH, w - j)
                        diag = L.causal and k0 + j + cols == (t + 1) * P
                        mm = pe.matmul(ps[:, b + j // CH, 0:cols], M1[p][:, t * P:(t + 1) * P],
                                       S1[p][:, k0 + j:k0 + j + cols], start=True, stop=not diag)
                        if diag:
                            mm = pe.matmul(ps[:, b + j // CH, cols - P:cols], identb[:], maskqsb[:],
                                           start=False, stop=True)
                    mm.then_inc(s["sc_ready"], 1)

                def values(n, p, k):
                    c, two = L.steps[k]
                    if k == L.first[c]:
                        at_least(pe, s["o_ready"], NC * n + c)
                    pe.wait_ge(s["p_ready"], 2 * K * n + 2 * k + 2)
                    for h2, (j, q0, _, _) in enumerate(two):
                        mm = pe.matmul(ps[h2 * DH:(h2 + 1) * DH, OUT, q0:CH], V[p][:, j, :],
                                       work[:, (2 * K * p + 2 * k + h2) % SLOTS, q0:CH],
                                       start=(k == L.first[c]), stop=(k + 1 == L.end[c]), skip_group_check=True)
                    mm.then_inc(s["pv_done"], 1)

                def stage(i, p, main, prep, tail):
                    n = 2 * i + p
                    jobs = L.jobs(i, p, main, prep, tail)
                    if main:
                        released("mt", n, 0)
                        if p == 0:
                            released("v", i, NC - 1)
                        if tail:
                            released("op", n - 1, NC - 2)
                    last = None
                    for k in range(K):
                        for at, kind, h, c, hp in jobs:
                            if at == k:
                                if last:
                                    released(*last)
                                job(kind, h, c, hp)
                                last = (kind, h, c)
                        if main:
                            if k == 0:
                                pe.wait_ge(s["dup_done"], 32 * n + 32)
                                pe.wait_ge(s["mrow_done"], 32 * n + 16)
                                pe.wait_ge(s["v_ready"] if p == 0 else s["vcopy_done"],
                                           8 * i + 8 if p == 0 else 16 * i + 16)
                            if k == L.first[NC // 2]:
                                pe.wait_ge(s["mrow_done"], 32 * n + 32)
                            for h2 in range(2):
                                scores(n, p, k, h2)
                        if prep:
                            for m in L.at_step(k):
                                maximum(n + 1, 1 - p, m)
                        if main and k >= 1:
                            values(n, p, k - 1)
                    if main:
                        values(n, p, K - 1)

                each_stage(pe.Fori, stage)
                released("op", HEADS - 1, NC - 2)
                job("den", HEADS - 1, NC - 1, 1)
                released("den", HEADS - 1, NC - 1)
                job("op", HEADS - 1, NC - 1, 1)

            def experts():
                pe.wait_ge(yt_ready, 2 * NC)
                pe.wait_ge(const_in, 16 * N_CONST)
                for t in range(NT):
                    mm = pe.matmul(ps[:, 0, t * E_EXP:(t + 1) * E_EXP], yv[:, t * P:(t + 1) * P], wg[:],
                                   start=True, stop=True)
                mm.then_inc(lg_ready, 1)
                pe.wait_ge(mask_ready, 1)
                m = small[:, 4, :, :].rearrange("p t e -> p (t e)")
                pe.matmul(ps[:, 1, 0:P], before[:], m, start=True, stop=True)
                pe.matmul(ps[:, 2, 0:P], ones[:], m, start=True, stop=True).then_inc(loc_psum, 1)
                pe.wait_ge(cf_ready, 1)
                for t in range(NT):
                    pe.transpose(ps[0:E_EXP, 3 + t % 2, 0:P], small[:, 5, t, :], ident[:]).then_inc(cT_psum, 1)
                    if t >= 1:
                        expert_tile(t - 1)
                expert_tile(NT - 1)

            def expert_tile(t):
                if t >= 2:
                    pe.wait_ge(x_exp, E_EXP * (t - 2) + E_EXP)
                b0 = 6 if t % 2 == 0 else 0
                for k in range(2):
                    pe.matmul(bank(b0 + k), yv[:, t * P:(t + 1) * P],
                              wexp[:, 4 * k:4 * k + 4, :].rearrange("p e f -> p (e f)"), start=True, stop=True)
                pe.wait_ge(cT_ready, t + 1)
                pe.matmul(ps[:, 5 if t % 2 == 0 else 2, 0:D], coefT[:, t % 2, :], bexp[:], start=True, stop=True).then_inc(xp_psum, 1)

            def channel_mix():
                for c in range(NC):
                    pe.wait_ge(mix_ready, 2 * c + 2)
                    if c >= 2:
                        pe.wait_ge(r_ready, c - 1)
                        pe.wait_ge(kr_ready, c - 1)
                    for t in range(TPC):
                        mm = pe.matmul(ps[:, c % 2, t * P:(t + 1) * P],
                                       work[:, c, t * P:(t + 1) * P], wmix[:, 0, :],
                                       start=True, stop=True)
                    mm.then_inc(r_psum, 1)
                    pe.matmul(bank(2 + c % 2), wmix[:, 1, :], work[:, 4 + c, :], start=True, stop=True).then_inc(k_psum, 1)
                    if c >= 1:
                        mix_out(c - 1)
                mix_out(NC - 1)

            def mix_out(c):
                pe.wait_ge(k_ready, c + 1)
                for t in range(TPC):
                    mm = pe.matmul(ps[:, 4 + c, t * P:(t + 1) * P], work[:, 4 + c, t * P:(t + 1) * P], wmix[:, 2, :],
                                   start=True, stop=True)
                mm.then_inc(mo_psum, 1)

            def l2_attention():
                pe.matmul(ps[:, 4, 0:D], wl2[:, 0, :], wl2[:, 1, :], start=True, stop=True).then_inc(l2_psum, 1)
                pe.wait_ge(l2_ready, 1)
                pe.matmul(ps[:, 5, 0:D], l2[:, 0, :], wl2[:, 2, :], start=True, stop=True).then_inc(l2_psum, 1)
                pe.wait_ge(l2_ready, 2)
                pe.matmul(ps[:, 6, 0:D], l2[:, 1, :], wl2[:, 3, :], start=True, stop=True).then_inc(l2_psum, 1)
                pe.wait_ge(l2_ready, 3)
                for c in range(NC):
                    pe.wait_ge(yt_ready, 4 * NC + c + 1)
                    for t in range(TPC):
                        mm = pe.matmul(ps[:, c, t * P:(t + 1) * P], yv[:, (c * TPC + t) * P:(c * TPC + t + 1) * P],
                                       l2[:, 2, :], start=True, stop=True)
                    mm.then_inc(lo_psum, 1)

            def mlp(n, k):
                s = F[n]
                for c in range(NC):
                    pe.wait_ge(yt_ready, k * NC + c + 1)
                    for j in range(NJ):
                        m = c * NJ + j
                        if m >= 4:
                            pe.wait_ge(s["h_ready"], m - 3)
                        else:
                            pe.wait_ge(yt_ready, k * NC + m + 1)
                        pe.matmul(bank(m % 4), wm[:, 2 * n, j * P:(j + 1) * P], yv[:, c * CH:(c + 1) * CH],
                                  start=True, stop=True).then_inc(s["h_psum"], 1)
                    if c >= 1:
                        mlp_out(n, c - 1)
                mlp_out(n, NC - 1)

            def mlp_out(n, c):
                s = F[n]
                pe.wait_ge(s["h_ready"], NJ * (c + 1))
                for t in range(TPC):
                    for j in range(NJ):
                        mm = pe.matmul(ps[:, 4 + c, t * P:(t + 1) * P], work[:, j * 4 + c, t * P:(t + 1) * P],
                                       wm[:, 2 * n + 1, j * P:(j + 1) * P], start=(j == 0), stop=(j == NJ - 1))
                mm.then_inc(s["f_psum"], 1)

            def weights():
                pe.wait_ge(gam_in, 1)
                pe.matmul(ps[:, 0, 0:2], ones[:], gam[:, 0:2], start=True, stop=True).then_inc(gam_psum, 1)
                pe.wait_ge(wm_ready, 2)
                for m in range(2):
                    for j in range(NJ):
                        mm = pe.transpose(ps[:, 1 + m, j * P:(j + 1) * P], work[:, 4 + m, j * P:(j + 1) * P], ident[:])
                    mm.then_inc(wT_psum, 1)

            def features():
                pe.wait_ge(fw_ready, 1)
                pe.transpose(ps[0:NF, 7, 0:HEADS], faw[:, 0:NF], ident[0:HEADS, 0:HEADS]).then_inc(fwT_psum, 1)
                pe.wait_ge(yt_ready, 7 * NC)
                for c in range(NC):
                    for m in range(3):
                        M = P if m < 2 else FH
                        if c >= 1:
                            pe.wait_ge(ft_ready, 4 * (c - 1) + m + 1)
                        pe.matmul(ps[0:M, m, :], wext[:, m * P:m * P + M], yv[:, c * CH:(c + 1) * CH],
                                  start=True, stop=True).then_inc(ft_psum, 1)
                    pe.wait_ge(ft_ready, 4 * c + 3)
                    for m in range(3):
                        M = P if m < 2 else FH
                        mm = pe.matmul(ps[0:NF, 3, :], w2b[0:M, m, :], work[0:M, m, :], start=(m == 0), stop=(m == 2))
                    mm.then_inc(ft_psum, 1)
                    pe.wait_ge(ft_ready, 4 * c + 4)
                    pe.wait_ge(fwT_ready, 1)
                    if c >= 1:
                        pe.wait_ge(br_ready, c)
                    pe.matmul(ps[0:HEADS, 4, :], fawT[:], fs[:], start=True, stop=True).then_inc(br_psum, 1)

            pe.wait_ge(const_in, 16 * N_CONST)
            pe.wait_ge(consts_ready, 1)
            weights()
            layernorm(0)
            pe.wait_ge(aux_ready, 1)
            pe.wait_ge(yt_ready, NC)
            attention(LAYERS[0])
            layernorm(1)
            pe.wait_ge(yt_ready, 2 * NC)
            experts()
            layernorm(2)
            pe.wait_ge(yt_ready, 3 * NC)
            attention(LAYERS[1])
            layernorm(3)
            channel_mix()
            layernorm(4)
            l2_attention()
            layernorm(5)
            mlp(0, 5)
            layernorm(6)
            features()
            pe.wait_ge(aux_ready, 2)
            attention(LAYERS[2])
            layernorm(7)
            mlp(1, 7)

        @block.scalar
        def _(act):
            def layernorm(k):
                act.wait_ge(var_ready, k + 1)
                act.activation(sd[:], stats[:, :, 0], ACT.Sqrt).then_inc(sd_ready, 1)
                for c in range(NC):
                    act.wait_ge(yt_psum, k * NC + c + 1)
                    act.activation(yv[:, c * CH:(c + 1) * CH], bank(c), ACT.Copy).then_inc(yt_ready, 1)

            def attention(L):
                s = A[L.n]
                K, NM = L.K, L.NM

                def copy_out(h, c):
                    act.wait_ge(s["pv_done"], K * h + L.end[c])
                    at_least(act, s["op_ready"], NC * h + c - 1)
                    act.activation(oT[:, c % 2, :], bank(OUT), ACT.Copy).then_inc(s["o_ready"], 1)

                def stage(i, p, main, prep, tail):
                    n = 2 * i + p
                    m_, q = n + 1, 1 - p
                    for k in range(K):
                        if tail and k == 0:
                            copy_out(n - 1, NC - 1)
                        if prep and k in L.qk_at:
                            c = L.qk_at.index(k)
                            act.wait_ge(s["proj_ready"], NC * m_ + c + 1)
                            for r, dst in ((slice(0, DH), M1[q]), (slice(DH, P), S1[q])):
                                act.activation(dst[0:DH, c * CH:(c + 1) * CH], ps[r, MISC, :], ACT.Identity,
                                               bias=bqk[r, q:q + 1]).then_inc(s["hi_ready"], 1)
                        if main:
                            for c in range(NC - 1):
                                if k == L.end[c] + 1:
                                    copy_out(n, c)
                            for h2 in range(2):
                                q0 = L.steps[k][1][h2][1]
                                e = 2 * k + h2
                                act.wait_ge(s["st_ready"], 2 * K * n + e + 1)
                                at_least(act, s["acc_ready"], 2 * K * n + e - SLOTS + 1)
                                at_least(act, s["pv_done"], K * n + k - SLOTS // 2 + 1)
                                act.activation(work[:, (2 * K * p + e) % SLOTS, q0:CH], ps[:, h2, q0:CH], ACT.Exp,
                                               scale=L.scale).then_inc(s["p_ready"], 1)
                        if prep:
                            for m in L.at_step(k):
                                w = L.maxima[m][2]
                                act.wait_ge(s["sc_ready"], NM * m_ + m + 1)
                                at_least(act, s["scan_ready"], NM * m_ + m - 1)
                                b = 4 + 2 * (m % 2)
                                flat = ps[:, b:b + 2, :].rearrange("p b k -> p (b k)")
                                act.activation(smax[:, m % 2, 0:w // 2], flat[:, w // 2:w], ACT.Copy)\
                                    .then_inc(s["cp_ready"], 1)

                each_stage(act.Fori, stage)
                copy_out(HEADS - 1, NC - 1)

            layernorm(0)
            attention(LAYERS[0])
            layernorm(1)
            act.wait_ge(dl_ready, 1)
            act.activation(small[:, 2, :, :], small[:, 1, :, :], ACT.Exp).then_inc(ex_ready, 1)
            for t in range(NT):
                act.wait_ge(cT_psum, t + 1)
                if t >= 2:
                    act.wait_ge(xp_psum, t - 1)
                act.activation(coefT[:, t % 2, :], ps[0:E_EXP, 3 + t % 2, 0:P], ACT.Copy).then_inc(cT_ready, 1)
            layernorm(2)
            attention(LAYERS[1])
            layernorm(3)
            for c in range(NC):
                act.wait_ge(r_psum, c + 1)
                act.activation(work[:, 8 + c, :], bank(c % 2), ACT.Sigmoid).then_inc(r_ready, 1)
                act.wait_ge(k_psum, c + 1)
                act.activation(work[:, 12 + c, :], bank(2 + c % 2), ACT.Relu).then_inc(kr_ready, 1)
            layernorm(4)
            layernorm(5)
            for m in range(NC * NJ):
                act.wait_ge(F[0]["h_psum"], m + 1)
                c, j = m // NJ, m % NJ
                act.activation(work[:, j * 4 + c, :], bank(m % 4), ACT.Relu, bias=b1[:, 0, j:j + 1]).then_inc(F[0]["h_ready"], 1)
            layernorm(6)
            act.wait_ge(fw_in, 1)
            act.activation(faw[:, 0:NF], faw[:, 0:NF], ACT.Exp).then_inc(fw_exp, 1)
            for c in range(NC):
                for m in range(3):
                    M = P if m < 2 else FH
                    act.wait_ge(ft_psum, 4 * c + m + 1)
                    if c >= 1:
                        act.wait_ge(ft_psum, 4 * c)
                    act.activation(work[0:M, m, :], ps[0:M, m, :], ACT.Gelu, bias=bext[0:M, m:m + 1]).then_inc(ft_ready, 1)
                act.wait_ge(ft_psum, 4 * c + 4)
                act.activation(fs[:], ps[0:NF, 3, :], ACT.Sigmoid, bias=b2ext[:]).then_inc(ft_ready, 1)
                act.wait_ge(br_psum, c + 1)
                if c >= 1:
                    act.wait_ge(br_out, 16 * c)
                act.activation(brow[:], ps[0:HEADS, 4, :], ACT.Copy, scale=1.0 / LAYERS[2].scale).then_inc(br_ready, 1)
            attention(LAYERS[2])
            layernorm(7)
            for m in range(NC * NJ):
                act.wait_ge(F[1]["h_psum"], m + 1)
                c, j = m // NJ, m % NJ
                act.activation(work[:, j * 4 + c, :], bank(m % 4), ACT.Gelu, bias=b1[:, 1, j:j + 1]).then_inc(F[1]["h_ready"], 1)

        @block.gpsimd
        def _(pool):
            def attention(L):
                s = A[L.n]

                def stage(i, p, main, prep, tail):
                    if not prep:
                        return
                    h = 2 * i + p + 1
                    for m, (t, _, w, final) in enumerate(L.maxima):
                        if final:
                            pool.wait_ge(s["scan_ready"], L.NM * h + m + 1)
                            pool.tensor_tensor(mcol[:, t:t + 1], scan[:, m % 2, w // 2 - 1:w // 2], zcol[:],
                                               ALU.add).then_inc(s["mcol_ready"], 1)

                each_stage(pool.Fori, stage)

            for L in LAYERS:
                attention(L)

        @block.vector
        def _(dve):
            steps = [0]

            def link(ins):
                steps[0] += 1
                ins.then_inc(dve_step, 1)
                dve.wait_ge(dve_step, steps[0])

            def layernorm(k, bias=None):
                for t in range(NT):
                    ins = dve.bn_stats(stats[:, t, :], x[:, t, :])
                link(ins)
                for t in range(NT):
                    ins = dve.bn_aggr(mv[:, t, :], stats[:, t, :])
                link(ins)
                dve.tensor_scalar(stats[:, :, 0], mv[:, :, 1], EPS, None, ALU.add).then_inc(var_ready, 1)
                dve.wait_ge(sd_ready, k + 1)
                link(dve.reciprocal(rstd[:], sd[:]))
                for t in range(NT):
                    ins = dve.tensor_scalar(work[:, t // TPC, (t % TPC) * P:(t % TPC + 1) * P], x[:, t, :],
                                            mv[:, t, 0:1], rstd[:, t:t + 1], ALU.subtract, ALU.mult)
                    ins.then_inc(yn_ready, 1)
                if bias is not None:
                    dve.wait_ge(yn_ready, (k + 1) * NT)
                    link(dve.tensor_tensor(x[:], x[:], obias[:, bias:bias + 1, :].to_broadcast([P, NT, D]), ALU.add))

            def attention(L):
                s = A[L.n]
                K, NM = L.K, L.NM

                def job(kind, h, c, p):
                    if kind == "qk":
                        for r, qk in ((slice(0, DH), 0), (slice(DH, P), 1)):
                            dve.wait_ge(s["hi_ready"], 8 * h + 2 * c + qk + 1)
                            hi = (M1, S1)[qk][p][0:DH, c * CH:(c + 1) * CH]
                            lo = (M2[p][0:DH], S2[p][DH:P])[qk][:, c * CH:(c + 1) * CH]
                            dve.scalar_tensor_tensor(lo, ps[r, MISC, :], bqk[r, p:p + 1], hi.bitcast(F32),
                                                     ALU.add, ALU.subtract).then_inc(s["lo_ready"], 1)
                    elif kind == "v":
                        dve.wait_ge(s["v_psum"], NC * h + c + 1)
                        at_least(dve, s["pv_done"], 2 * K * h - K)
                        at_least(dve, s["vcopy_done"], 16 * h)
                        for half, dst in enumerate((V[0], Vnext)):
                            cols = slice(half * DH, (half + 1) * DH)
                            dve.tensor_tensor(dst[:, c * TPC:(c + 1) * TPC, :],
                                              bank(MISC).rearrange("p (t d) -> p t d", d=P)[:, :, cols],
                                              bv[:, cols].rearrange("p (o d) -> p o d", o=1).to_broadcast([P, TPC, DH]),
                                              ALU.add).then_inc(s["v_ready"], 1)
                    elif kind == "mt":
                        dve.wait_ge(s["mt_psum"], 2 * h + c + 1)
                        at_least(dve, s["mrow_done"], 32 * h + 16 * c - 16)
                        dve.tensor_scalar(mT[:, c, :], ps[0:NT // 2, MISC, 0:P], -1.0, None, ALU.mult)\
                            .then_inc(s["mt_ready"], 1)
                    elif kind == "den":
                        dve.wait_ge(s["den_ready"], NC * h + c + 1)
                        dve.reciprocal(rinv[:, c % 2, :], bank(MISC).rearrange("p (t d) -> p t d", d=P)[:, :, 0])\
                            .then_inc(s["rinv_ready"], 1)
                    else:
                        dve.wait_ge(s["op_ready"], NC * h + c + 1)
                        dve.wait_ge(s["rinv_ready"], NC * h + c + 1)
                        for t in range(TPC):
                            xt = x[:, c * TPC + t, :]
                            dve.scalar_tensor_tensor(xt, ps[:, MISC, t * P:(t + 1) * P], rinv[:, c % 2, t:t + 1], xt,
                                                     ALU.mult, ALU.add).then_inc(s["x_added"], 1)

                def add(n, p, k):
                    c, two = L.steps[k]
                    for h2, (_, q0, _, _) in enumerate(two):
                        e = 2 * k + h2
                        o = acc[:, c % 2, q0:CH]
                        tile = work[:, (2 * K * p + e) % SLOTS, q0:CH]
                        dve.wait_ge(s["p_ready"], 2 * K * n + e + 1)
                        if e == 2 * L.first[c]:
                            at_least(dve, s["den_ready"], NC * n + c - 1)
                            dve.tensor_copy(o, tile).then_inc(s["acc_ready"], 1)
                        else:
                            dve.wait_ge(s["acc_ready"], 2 * K * n + e)
                            dve.tensor_tensor(o, o, tile, ALU.add).then_inc(s["acc_ready"], 1)

                def maximum(h, m):
                    t, k0, w, _ = L.maxima[m]
                    dve.wait_ge(s["cp_ready"], NM * h + m + 1)
                    at_least(dve, s["mcol_ready"], NT * h + L.finals(m - 1))
                    at_least(dve, s["scan_ready"], NM * h + m)
                    start = LOWEST
                    if k0:
                        start = scan[:, (m - 1) % 2, CH - 1:CH]
                    b = 4 + 2 * (m % 2)
                    flat = ps[:, b:b + 2, :].rearrange("p b k -> p (b k)")
                    dve.tensor_tensor_scan(scan[:, m % 2, 0:w // 2], flat[:, 0:w // 2], smax[:, m % 2, 0:w // 2],
                                           start, ALU.max, ALU.max).then_inc(s["scan_ready"], 1)

                def stage(i, p, main, prep, tail):
                    n = 2 * i + p
                    jobs = L.jobs(i, p, main, prep, tail)
                    for k in range(K):
                        for at, kind, h, c, hp in jobs:
                            if at == k:
                                job(kind, h, c, hp)
                        if main:
                            add(n, p, k)
                        if prep:
                            for m in L.at_step(k):
                                maximum(n + 1, m)

                each_stage(dve.Fori, stage)
                job("den", HEADS - 1, NC - 1, 1)
                job("op", HEADS - 1, NC - 1, 1)
                dve.wait_ge(s["x_added"], NT * HEADS)

            def abs_sum(o, w):
                return dve.tensor_reduce(o, w, AX.X, ALU.add, apply_absolute_value=True)

            def weights():
                dve.wait_ge(const_in, 16 * N_CONST)
                for m in range(2):
                    ins = abs_sum(gam[:, m:m + 1], wt[:, m, :])
                ins.then_inc(gam_in, 1)
                for m in range(2):
                    w = wt[:, 2 + m, :]
                    n = NJ if m == 0 else 1
                    k = FF // n
                    wr = w.rearrange("p (n k) -> p n k", n=n)
                    link(abs_sum(few[:, m, 0:n], wr))
                    link(dve.tensor_scalar(few[:, 2 + m, 0:n], few[:, m, 0:n], 1.0 / k, None, ALU.mult))
                    link(dve.tensor_scalar(wtmp[:], w, 0.0, None, ALU.is_lt))
                    link(dve.scalar_tensor_tensor(work[:, 6, :], w, 0.0, wtmp[:], ALU.is_gt, ALU.subtract))
                    for q in range(n):
                        cs = slice(q * k, (q + 1) * k)
                        ins = dve.scalar_tensor_tensor(work[:, 7, cs], work[:, 6, cs], few[:, 2 + m, q:q + 1], w[:, cs],
                                                       ALU.mult, ALU.subtract)
                    link(ins)
                    dve.tensor_tensor(work[:, 4 + m, :], w, work[:, 7, :], ALU.add).then_inc(wm_ready, 1)
                    dve.wait_ge(wm_ready, m + 1)
                dve.wait_ge(gam_psum, 1)
                link(dve.tensor_scalar(gam[:, 2:4], ps[:, 0, 0:2], 1.0 / (FF * D), EPS, ALU.mult, ALU.add))
                link(dve.tensor_scalar(gam[:, 4:6], gam[:, 2:4], 0.5, None, ALU.mult))
                link(dve.tensor_scalar(gam[:, 6:8], gam[:, 2:4], -0.5, None, ALU.mult))
                for m in range(2):
                    link(dve.tensor_scalar(wtmp[:], wt[:, m, :], gam[:, 6 + m:7 + m], None, ALU.is_lt))
                    link(dve.scalar_tensor_tensor(wm[:, m, :], wt[:, m, :], gam[:, 4 + m:5 + m], wtmp[:],
                                                  ALU.is_gt, ALU.subtract))
                for m in range(2):
                    dve.wait_ge(wT_psum, m + 1)
                    link(dve.tensor_copy(wm[:, 2 + m, :], bank(1 + m)))

            def experts():
                def bc(v):
                    return v.rearrange("p (t o) -> p t o", o=1).to_broadcast([P, NT, E_EXP])
                sm = [small[:, n, :, :] for n in range(8)]
                fw = [few[:, n, :] for n in range(4)]
                dve.wait_ge(lg_ready, 1)
                lg = ps[:, 0, 0:P].rearrange("p (t e) -> p t e", e=E_EXP)
                link(dve.tensor_copy(sm[0], lg))
                link(dve.tensor_reduce(fw[0], sm[0], AX.X, ALU.max))
                dve.tensor_tensor(sm[1], sm[0], bc(fw[0]), ALU.subtract).then_inc(dl_ready, 1)
                dve.wait_ge(ex_ready, 1)
                link(dve.tensor_reduce(fw[1], sm[2], AX.X, ALU.add))
                link(dve.reciprocal(fw[2], fw[1]))
                link(dve.tensor_tensor(sm[3], sm[2], bc(fw[2]), ALU.mult))
                link(dve.tensor_reduce(fw[3], sm[3], AX.X, ALU.max))
                link(dve.tensor_tensor(sm[0], sm[3], bc(fw[3]), ALU.is_ge))
                link(dve.tensor_tensor(sm[1], sm[0], first[:].rearrange("p (o e) -> p o e", o=1)
                                       .to_broadcast([P, NT, E_EXP]), ALU.mult))
                link(dve.tensor_reduce(fw[0], sm[1], AX.X, ALU.max))
                dve.tensor_tensor(sm[4], sm[1], bc(fw[0]), ALU.is_equal).then_inc(mask_ready, 1)
                dve.wait_ge(loc_psum, 1)
                tot = ps[:, 2, 0:P].rearrange("p (t e) -> p t e", e=E_EXP)
                link(dve.tensor_copy(sm[6], tot))
                src, dst = 6, 7
                for k in (1, 2, 4, 8):
                    link(dve.tensor_tensor(sm[dst][:, k:NT, :], sm[src][:, k:NT, :], sm[src][:, 0:NT - k, :], ALU.add))
                    link(dve.tensor_copy(sm[dst][:, 0:k, :], sm[src][:, 0:k, :]))
                    src, dst = dst, src
                link(dve.tensor_tensor(sm[0], sm[src], tot, ALU.subtract))
                link(dve.tensor_tensor(sm[1], sm[0], ps[:, 1, 0:P].rearrange("p (t e) -> p t e", e=E_EXP), ALU.add))
                link(dve.tensor_scalar(sm[2], sm[1], float(CAP), None, ALU.is_lt))
                link(dve.tensor_tensor(sm[0], sm[2], sm[4], ALU.mult))
                dve.tensor_tensor(sm[5], sm[0], sm[3], ALU.mult).then_inc(cf_ready, 1)
                dve.wait_ge(cf_ready, 1)
                for t in range(NT):
                    dve.wait_ge(xp_psum, t + 1)
                    b0 = 6 if t % 2 == 0 else 0
                    link(dve.tensor_tensor(x[:, t, :], x[:, t, :], ps[:, 5 if t % 2 == 0 else 2, 0:D], ALU.add))
                    for e in range(E_EXP):
                        dve.scalar_tensor_tensor(x[:, t, :], ps[:, b0 + e // 4, (e % 4) * D:(e % 4 + 1) * D],
                                                 sm[5][:, t, e:e + 1], x[:, t, :], ALU.mult, ALU.add).then_inc(x_exp, 1)
                        dve.wait_ge(x_exp, t * E_EXP + e + 1)

            def channel_mix():
                dve.wait_ge(yt_ready, 4 * NC)
                for c in range(NC):
                    cur = yT[:, 1 + c * CH:1 + (c + 1) * CH]
                    prev = yT[:, c * CH:(c + 1) * CH]
                    for m in range(2):
                        link(dve.tensor_scalar(mixed[:], cur, mu[:, m:m + 1], None, ALU.mult))
                        t1 = mixed[:]
                        dve.scalar_tensor_tensor(work[:, 4 * m + c, :], prev, mu[:, 2 + m:3 + m], t1,
                                                 ALU.mult, ALU.add).then_inc(mix_ready, 1)
                        dve.wait_ge(mix_ready, 2 * c + m + 1)
                for c in range(NC):
                    dve.wait_ge(kr_ready, c + 1)
                    dve.tensor_tensor(work[:, 4 + c, :], work[:, 12 + c, :], work[:, 12 + c, :], ALU.mult).then_inc(k_ready, 1)
                for c in range(NC):
                    dve.wait_ge(mo_psum, c + 1)
                    dve.wait_ge(r_ready, c + 1)
                    link(dve.tensor_tensor(work[:, 12 + c, :], bank(4 + c), work[:, 8 + c, :], ALU.mult))
                    xs = x[:, c * TPC:(c + 1) * TPC, :]
                    link(dve.tensor_tensor(xs, xs, work[:, 12 + c, :].rearrange("p (t d) -> p t d", d=D), ALU.add))

            def l2_attention():
                dve.wait_ge(l2_psum, 1)
                dve.scalar_tensor_tensor(l2[:, 0, :], ps[:, 4, 0:D], float(8) ** -0.5, wl2[:, 4, :],
                                         ALU.mult, ALU.mult).then_inc(l2_ready, 1)
                for m in range(2):
                    dve.wait_ge(l2_psum, 2 + m)
                    dve.tensor_copy(l2[:, 1 + m, :], ps[:, 5 + m, 0:D]).then_inc(l2_ready, 1)
                add_out(lo_psum, 0)

            def add_out(ready, b0, done=None):
                for c in range(NC):
                    dve.wait_ge(ready, c + 1)
                    xs = x[:, c * TPC:(c + 1) * TPC, :]
                    ins = dve.tensor_tensor(xs, xs, bank(b0 + c).rearrange("p (t d) -> p t d", d=D), ALU.add)
                    if done is not None:
                        ins.then_inc(done, 1)
                    else:
                        link(ins)

            def features():
                link(dve.tensor_reduce(faw[:, 5:6], faw[:, 0:NF], AX.X, ALU.max))
                dve.tensor_scalar(faw[:, 0:NF], faw[:, 0:NF], faw[:, 5:6], None, ALU.subtract).then_inc(fw_in, 1)
                dve.wait_ge(fw_exp, 1)
                link(dve.tensor_reduce(faw[:, 6:7], faw[:, 0:NF], AX.X, ALU.add))
                link(dve.reciprocal(faw[:, 7:8], faw[:, 6:7]))
                dve.tensor_scalar(faw[:, 0:NF], faw[:, 0:NF], faw[:, 7:8], None, ALU.mult).then_inc(fw_ready, 1)
                dve.wait_ge(fwT_psum, 1)
                dve.tensor_copy(fawT[:], ps[0:NF, 7, 0:HEADS]).then_inc(fwT_ready, 1)

            def auxiliary_rows():
                dve.wait_ge(aux_in, 16)
                aux = work[:, 8:8 + NC, :].rearrange("p c q -> p (c q)")
                for h in range(2):
                    dve.tensor_copy(S1[h][DH:P, :], aux[DH:P, :])
                    ins = dve.tensor_copy(M1[h][DH:P, :], aux[0:DH, :])
                ins.then_inc(aux_ready, 1)
                dve.wait_ge(aux_ready, 2)

            for h in range(2):
                for m in (M1[h], S1[h]):
                    ins = dve.memset(m[DH:P, :].bitcast(F32), 0.0)
            link(ins)
            for h in range(2):
                ins = dve.memset(S1[h][ROW_M:ROW_M + 1, :].bitcast(F32), 1.0)
            ins.then_inc(aux_ready, 1)
            dve.memset(yT[:, 0:1], 0.0)
            dve.memset(zcol[:], 0.0)
            dve.memset(zrow[:], 0.0)
            dve.memset(ones[:], 1.0).then_inc(consts_ready, 1)
            weights()
            for dst, src in ((identb, ident), (maskqsb, maskqs), (masksqb, masksq)):
                dve.tensor_copy(dst[:], src[:])
            dve.memset(allb[:], -BIG)
            dve.tensor_scalar(mu[:, 2:4], mu[:, 0:2], -1.0, 1.0, ALU.mult, ALU.add)
            for m in range(3):
                dve.tensor_scalar(w2b[:, m, :], w2m[:, m, :], w2ext[:, m:m + 1], None, ALU.mult)
            dve.wait_ge(x_in, 16)
            layernorm(0, bias=0)
            attention(LAYERS[0])
            layernorm(1)
            experts()
            link(dve.memset(bqk[:], 0.0))
            link(dve.memset(bv[:], 0.0))
            layernorm(2, bias=1)
            attention(LAYERS[1])
            layernorm(3)
            channel_mix()
            layernorm(4, bias=2)
            l2_attention()
            layernorm(5, bias=3)
            add_out(F[0]["f_psum"], 4)
            layernorm(6, bias=4)
            features()
            auxiliary_rows()
            attention(LAYERS[2])
            layernorm(7, bias=5)
            add_out(F[1]["f_psum"], 4, done=F[1]["f_used"])


def constants():
    f = np.float32
    i = np.arange(P)
    c = {"c_ident": np.eye(P, dtype=f)}
    c["c_maskqs"] = np.where(i[None, :] > i[:, None], f(-BIG), f(0))
    c["c_masksq"] = np.ascontiguousarray(c["c_maskqs"].T)
    c["c_before"] = (i[:, None] < i[None, :]).astype(f)
    c["c_first"] = np.tile(E_EXP - np.arange(E_EXP, dtype=f), (P, 1))
    c["c_block"] = (i[:, None] // 8 == i[None, :] // 8).astype(f)
    h = np.arange(3 * P).reshape(3, P).T
    c["c_w2m"] = (h[:, :, None] // FH == np.arange(NF)).astype(f)
    allowed = np.zeros((T, T), bool)
    for r, chans in enumerate(REGIONS):
        ch = [k + 6 for k in chans]
        allowed[r, ch] = True
        allowed[ch, r] = True
    allowed[:NREG, :NREG] = True
    allowed[NREG:, NREG:] = True
    keys, queries = np.zeros((DH, T), f), np.zeros((DH, T), f)
    keys[ROW_M - DH] = keys[ROW_B - DH] = 1
    for r in range(NREG):
        keys[ROW_R - DH + r, r] = 1
        queries[ROW_R - DH + r] = np.where(allowed[:, r], 0, -BIG)
        keys[ROW_C - DH + r, NREG:] = np.where(allowed[r, NREG:], 0, 1)
        queries[ROW_C - DH + r, r] = -BIG
    c["c_aux"] = np.concatenate([queries, keys])
    return c


def laid_out(i):
    flat = lambda w: np.ascontiguousarray(w.reshape(HEADS * DH, D).T)
    d = {k: i[k] for k in (
        "L0_attn_x", "L0_attn_b_O", "L1_attn_b_u", "L2_attn_out_b", "L2_ffn_b2", "L3_attn_out_b", "L3_ffn_b2",
        "L0_ffn_wg", "L0_ffn_b", "L1_ffn_mu_r", "L1_ffn_mu_k", "L1_attn_w_u", "L3_attn_out_w", "L3_attn_ext_b2", "L3_attn_faw")}
    by_head = lambda q, k: np.stack([q.reshape(D, HEADS, DH), k.reshape(D, HEADS, DH)], 2).reshape(D, -1)
    q3, k3, d["wv_2"] = np.split(i["L3_attn_qkv_w"], 3, axis=1)
    d["wqk_0"] = by_head(flat(i["L0_attn_W_Q"]), flat(i["L0_attn_W_K"]))
    d["wqk_1"] = by_head(i["L1_attn_w_q"], i["L1_attn_w_k"])
    d["wqk_2"] = by_head(q3, k3)
    d["wv_0"], d["wv_1"] = flat(i["L0_attn_W_V"]), i["L1_attn_w_v"]
    d["L0_wo"] = i["L0_attn_W_O"].transpose(0, 2, 1).reshape(HEADS * DH, D)
    d["L0_bqk"] = np.stack([i["L0_attn_b_Q"], i["L0_attn_b_K"]], 1).reshape(-1, 1)
    d["L0_bv"] = i["L0_attn_b_V"].reshape(1, -1)
    d["L0_wexp"] = i["L0_ffn_W"].transpose(2, 0, 1)
    d["L1_wmix"] = np.stack([i["L1_ffn_W_r"].T, i["L1_ffn_W_k"].T, i["L1_ffn_W_v"].T], 1)
    q, v = i["L2_attn_q_weight"].reshape(D, D), i["L2_attn_v_weight"].reshape(D, D)
    d["L2_w"] = np.stack([q, v, q.T, i["L2_attn_out_w"].T], 1)
    tiles = lambda w: w.reshape(NJ, P, D).transpose(1, 0, 2).reshape(P, FF)
    d["mlp_w"] = np.stack([i["L2_ffn_W1"].T, tiles(i["L2_ffn_W2"].T), tiles(i["L3_ffn_w1"]), i["L3_ffn_w2"]], 1)
    d["mlp_b1"] = np.stack([i["L2_ffn_b1"].reshape(NJ, P).T, i["L3_ffn_b1"].reshape(NJ, P).T], 1)
    d["L3_wext"] = i["L3_attn_ext_w1"].transpose(1, 0, 2).reshape(D, NF * FH)

    def hidden(w):
        o = np.zeros((3 * P,), np.float32)
        o[:NF * FH] = w.reshape(-1)
        return o.reshape(3, P).T
    d["L3_bext"], d["L3_w2ext"] = hidden(i["L3_attn_ext_b1"]), hidden(i["L3_attn_ext_w2"])
    return d


def kernel(**inputs):
    import concourse.bacc as bacc
    from concourse.bass_utils import run_bass_kernel_spmd

    nc = bacc.Bacc("TRN2", target_bir_lowering=False, num_devices=1)
    inputs = {k: np.asarray(v) for k, v in inputs.items()}
    arrays, aps = {}, {}
    for name, v in {**laid_out(inputs), **constants()}.items():
        v = np.ascontiguousarray(v)
        arrays["in_" + name] = v
        aps[name] = nc.dram_tensor("in_" + name, v.shape, mybir.dt.from_np(v.dtype), kind="ExternalInput").ap()
    out = nc.dram_tensor("out_x", [1, T, D], F32, kind="ExternalOutput").ap()
    program(nc, aps, out)
    r = run_bass_kernel_spmd(nc, [arrays], core_ids=[0])
    return r.results[0]["out_x"]
```
